# Optimizing a Trainium2 kernel written in Bass

```python
import numpy as np
import jax
import jax.numpy as jnp

def _softmax(x, axis=-1):
    return jax.nn.softmax(x, axis=axis)

def _gelu(x):
    return jax.nn.gelu(x, approximate=True)

def _silu(x):
    return jax.nn.silu(x)

def _sigmoid(x):
    return jax.nn.sigmoid(x)

def _layernorm(x, axis=-1, eps=1e-05):
    m = jnp.mean(x, axis=axis, keepdims=True)
    v = jnp.var(x, axis=axis, keepdims=True)
    return (x - m) / jnp.sqrt(v + eps)

def _scatter_add(tgt, idx, src, axis=0):
    return tgt.at[idx].add(src)

def _segment_sum(src, seg, n):
    return jax.ops.segment_sum(src, seg, n)
kernel_name = 'mk_vit_tower_d1_tok_img256_r4_30f2f9'

def setup_inputs(seed: int=0):
    np.random.seed(seed)
    _w = jnp.asarray

    def _rec_inputs():
        import jax
        import jax.numpy as jnp
        _rk = jax.random.key(seed)
        x = -0.000125008 + 0.999885 * jax.random.normal(jax.random.fold_in(_rk, 1), (4, 64, 64, 64), jnp.float32)
        return x
    x = _rec_inputs()

    def _L0_tok_setup():
        import jax, jax.numpy as jnp
        import numpy as np
        DIM = 64
        NH = 8
        WH, WW = (8, 8)

        def _rope_axis(x, axis):
            half = x.shape[-1]
            inv_freq = 1.0 / 10000.0 ** (jnp.arange(0, half, 2, dtype=jnp.float32) / half)
            pos = jnp.arange(x.shape[axis], dtype=jnp.float32)
            ang = pos[:, None] * inv_freq
            cos, sin = (jnp.cos(ang), jnp.sin(ang))
            shape = [1, 1, 1, ang.shape[-1]]
            shape[axis] = ang.shape[0]
            cos = cos.reshape(shape).astype(x.dtype)
            sin = sin.reshape(shape).astype(x.dtype)
            x1, x2 = (x[..., 0::2], x[..., 1::2])
            r1 = x1 * cos - x2 * sin
            r2 = x1 * sin + x2 * cos
            return jnp.stack([r1, r2], axis=-1).reshape(x.shape)

        def _rope2(x):
            half = x.shape[-1] // 2
            return jnp.concatenate([_rope_axis(x[..., :half], 1), _rope_axis(x[..., half:], 2)], axis=-1)
        key = jax.random.key(seed)
        ks = jax.random.split(key, 5)
        B, H, W, C = (32, 64, 64, DIM)
        s = 1.0 / np.sqrt(C)
        return {'x': jax.random.normal(ks[0], (B, H, W, C), dtype=jnp.float32), 'qkv_w': jax.random.uniform(ks[1], (3 * C, C), jnp.float32, -s, s), 'qkv_b': jax.random.uniform(ks[2], (3 * C,), jnp.float32, -s, s), 'proj_w': jax.random.uniform(ks[3], (C, C), jnp.float32, -s, s), 'proj_b': jax.random.uniform(ks[4], (C,), jnp.float32, -s, s)}
    _L0_tok_all = _L0_tok_setup()
    _L0_tok_in = {k: v for k, v in _L0_tok_all.items() if k in ('qkv_w', 'qkv_b', 'proj_w', 'proj_b')}
    del _L0_tok_all

    def _L0_attn_setup():
        import jax, jax.numpy as jnp
        import numpy as np
        B, L, DIN, DT_RANK, N = (4, 512, 64, 16, 16)

        def _selective_scan(u, delta, A, Bm, Cm, D):
            deltaA = jnp.einsum('bld,dn->bldn', delta, A)
            deltaBu = jnp.einsum('bld,bld,bln->bldn', delta, u, Bm)
            shifted = jnp.concatenate([deltaA[:, 1:], jnp.zeros_like(deltaA[:, :1])], axis=1)
            cum = jnp.exp(jnp.flip(jnp.cumsum(jnp.flip(shifted, axis=1), axis=1), axis=1))
            x = deltaBu * cum
            x = jnp.cumsum(x, axis=1) / (cum + 1e-12)
            out = jnp.einsum('bldn,bln->bld', x, Cm)
            return out + u * D
        key = jax.random.key(seed)
        k0, k1, k2 = jax.random.split(key, 3)
        inputs = jax.random.normal(k0, (B, L, DIN), dtype=jnp.float32)
        W_dbc = jax.random.normal(k1, (DIN, DT_RANK + 2 * N), dtype=jnp.float32) * 0.05
        W_dt = jax.random.normal(k2, (DT_RANK, DIN), dtype=jnp.float32) * 0.05
        b_dt = jnp.zeros((DIN,), dtype=jnp.float32)
        A_log = jnp.log(jnp.tile(jnp.arange(1, N + 1, dtype=jnp.float32)[None, :], (DIN, 1)))
        D = jnp.ones((DIN,), dtype=jnp.float32)
        return {'inputs': inputs, 'W_dbc': W_dbc, 'W_dt': W_dt, 'b_dt': b_dt, 'A_log': A_log, 'D': D}
    _L0_attn_all = _L0_attn_setup()
    _L0_attn_in = {k: v for k, v in _L0_attn_all.items() if k in ('W_dbc', 'W_dt', 'b_dt', 'A_log', 'D')}
    del _L0_attn_all

    def _L0_ffn_setup():
        import jax, jax.numpy as jnp
        import numpy as np
        B, K, D = (128, 16, 64)
        E = 32
        H = int(D * 0.25)
        key = jax.random.key(seed)
        ks = jax.random.split(key, 7)
        d_rs = D ** (-0.5)
        h_rs = H ** (-0.5)
        x = jax.random.normal(ks[0], (B, K, D), dtype=jnp.float32)
        router_w = jax.random.uniform(ks[1], (E, D), jnp.float32, -d_rs, d_rs)
        router_b = jax.random.uniform(ks[2], (E,), jnp.float32, -d_rs, d_rs)
        W1 = jax.random.uniform(ks[3], (E, D, H), jnp.float32, -h_rs, h_rs)
        b1 = jax.random.uniform(ks[4], (E, H), jnp.float32, -h_rs, h_rs)
        W2 = jax.random.uniform(ks[5], (E, H, D), jnp.float32, -d_rs, d_rs)
        b2 = jax.random.uniform(ks[6], (E, D), jnp.float32, -d_rs, d_rs)
        return {'x': x, 'router_w': router_w, 'router_b': router_b, 'W1': W1, 'b1': b1, 'W2': W2, 'b2': b2}
    _L0_ffn_all = _L0_ffn_setup()
    _L0_ffn_in = {k: v for k, v in _L0_ffn_all.items() if k in ('router_w', 'router_b', 'W1', 'b1', 'W2', 'b2')}
    del _L0_ffn_all
    return {'x': x, 'L0_tok_qkv_w': _L0_tok_in['qkv_w'], 'L0_tok_qkv_b': _L0_tok_in['qkv_b'], 'L0_tok_proj_w': _L0_tok_in['proj_w'], 'L0_tok_proj_b': _L0_tok_in['proj_b'], 'L0_attn_W_dbc': _L0_attn_in['W_dbc'], 'L0_attn_W_dt': _L0_attn_in['W_dt'], 'L0_attn_b_dt': _L0_attn_in['b_dt'], 'L0_attn_A_log': _L0_attn_in['A_log'], 'L0_attn_D': _L0_attn_in['D'], 'L0_ffn_router_w': _L0_ffn_in['router_w'], 'L0_ffn_router_b': _L0_ffn_in['router_b'], 'L0_ffn_W1': _L0_ffn_in['W1'], 'L0_ffn_b1': _L0_ffn_in['b1'], 'L0_ffn_W2': _L0_ffn_in['W2'], 'L0_ffn_b2': _L0_ffn_in['b2']}

def reference(x, L0_tok_qkv_w, L0_tok_qkv_b, L0_tok_proj_w, L0_tok_proj_b, L0_attn_W_dbc, L0_attn_W_dt, L0_attn_b_dt, L0_attn_A_log, L0_attn_D, L0_ffn_router_w, L0_ffn_router_b, L0_ffn_W1, L0_ffn_b1, L0_ffn_W2, L0_ffn_b2):
    import jax
    import jax.numpy as jnp

    def _L0_tok_ref(x, qkv_w, qkv_b, proj_w, proj_b):
        import jax, jax.numpy as jnp
        import numpy as np
        DIM = 64
        NH = 8
        WH, WW = (8, 8)

        def _rope_axis(x, axis):
            half = x.shape[-1]
            inv_freq = 1.0 / 10000.0 ** (jnp.arange(0, half, 2, dtype=jnp.float32) / half)
            pos = jnp.arange(x.shape[axis], dtype=jnp.float32)
            ang = pos[:, None] * inv_freq
            cos, sin = (jnp.cos(ang), jnp.sin(ang))
            shape = [1, 1, 1, ang.shape[-1]]
            shape[axis] = ang.shape[0]
            cos = cos.reshape(shape).astype(x.dtype)
            sin = sin.reshape(shape).astype(x.dtype)
            x1, x2 = (x[..., 0::2], x[..., 1::2])
            r1 = x1 * cos - x2 * sin
            r2 = x1 * sin + x2 * cos
            return jnp.stack([r1, r2], axis=-1).reshape(x.shape)

        def _rope2(x):
            half = x.shape[-1] // 2
            return jnp.concatenate([_rope_axis(x[..., :half], 1), _rope_axis(x[..., half:], 2)], axis=-1)
        B, H, W, C = x.shape
        hd = C // NH
        N = WH * WW
        xw = x.reshape(B, H // WH, WH, W // WW, WW, C).transpose(0, 1, 3, 2, 4, 5).reshape(-1, N, C)
        qkv = xw @ qkv_w.T + qkv_b
        qkv = qkv.reshape(-1, N, 3, NH, hd).transpose(2, 0, 3, 1, 4)
        q, k, v = (qkv[0], qkv[1], qkv[2])
        q = _rope2(q.reshape(-1, WH, WW, hd)).reshape(-1, NH, N, hd)
        k = _rope2(k.reshape(-1, WH, WW, hd)).reshape(-1, NH, N, hd)
        scale = hd ** (-0.5)
        attn = jax.nn.softmax(q * scale @ jnp.swapaxes(k, -2, -1), axis=-1)
        out = (attn @ v).transpose(0, 2, 1, 3).reshape(-1, N, C)
        out = out.reshape(B, H // WH, W // WW, WH, WW, C).transpose(0, 1, 3, 2, 4, 5).reshape(B, H * W, C)
        return out @ proj_w.T + proj_b

    def _L0_attn_ref(inputs, W_dbc, W_dt, b_dt, A_log, D):
        import jax, jax.numpy as jnp
        import numpy as np
        B, L, DIN, DT_RANK, N = (4, 512, 64, 16, 16)

        def _selective_scan(u, delta, A, Bm, Cm, D):
            deltaA = jnp.einsum('bld,dn->bldn', delta, A)
            deltaBu = jnp.einsum('bld,bld,bln->bldn', delta, u, Bm)
            shifted = jnp.concatenate([deltaA[:, 1:], jnp.zeros_like(deltaA[:, :1])], axis=1)
            cum = jnp.exp(jnp.flip(jnp.cumsum(jnp.flip(shifted, axis=1), axis=1), axis=1))
            x = deltaBu * cum
            x = jnp.cumsum(x, axis=1) / (cum + 1e-12)
            out = jnp.einsum('bldn,bln->bld', x, Cm)
            return out + u * D
        A = -jnp.exp(A_log)
        deltaBC = inputs @ W_dbc
        delta, Bm, Cm = jnp.split(deltaBC, [DT_RANK, DT_RANK + N], axis=-1)
        delta = jax.nn.softplus(delta @ W_dt + b_dt)
        return _selective_scan(inputs, delta, A, Bm, Cm, D)

    def _L0_ffn_ref(x, router_w, router_b, W1, b1, W2, b2):
        import jax, jax.numpy as jnp
        import numpy as np
        B, K, D = (128, 16, 64)
        E = 32
        H = int(D * 0.25)
        xf = x.reshape(-1, D)
        logits = xf @ router_w.T + router_b
        idx = jnp.argmax(logits, axis=-1)
        w1t = jnp.take(W1, idx, axis=0)
        h = jnp.einsum('nd,ndh->nh', xf, w1t) + jnp.take(b1, idx, axis=0)
        h = jax.nn.relu(h)
        w2t = jnp.take(W2, idx, axis=0)
        out = jnp.einsum('nh,nhd->nd', h, w2t) + jnp.take(b2, idx, axis=0)
        out = jax.nn.relu(out)
        return out.reshape(x.shape)
    h = _L0_tok_ref(x, L0_tok_qkv_w, L0_tok_qkv_b, L0_tok_proj_w, L0_tok_proj_b)
    h = h + _L0_attn_ref(_layernorm(h, axis=-1), L0_attn_W_dbc, L0_attn_W_dt, L0_attn_b_dt, L0_attn_A_log, L0_attn_D)
    h = h + _L0_ffn_ref(_layernorm(h, axis=-1), L0_ffn_router_w, L0_ffn_router_b, L0_ffn_W1, L0_ffn_b1, L0_ffn_W2, L0_ffn_b2)
    return h

_drawn_inputs = setup_inputs


def setup_inputs(seed=0):
    import zlib

    import numpy as np

    out = dict(_drawn_inputs(seed))
    spreads = {'L0_attn_b_dt': (0.0, 0.8), 'L0_attn_D': (1.0, 0.2)}
    factors = {'L0_attn_W_dbc': 2.701, 'L0_attn_W_dt': 8.0, 'L0_attn_A_log': 5.462, 'L0_ffn_b1': 3.674}
    for name, (base, spread) in spreads.items():
        noise = np.random.default_rng([zlib.crc32(name.encode()), seed]).standard_normal(out[name].shape)
        drawn = base * np.exp(spread * noise) if base else spread * noise
        out[name] = jnp.asarray(drawn.astype(out[name].dtype))
    for name, factor in factors.items():
        out[name] = (out[name] * factor).astype(out[name].dtype)
    return out
```

```python
from contextlib import ExitStack

import concourse.bass as bass
from concourse import mybir

F32 = mybir.dt.float32
I32 = mybir.dt.int32
ALU = mybir.AluOpType
ACT = mybir.ActivationFunctionType
AX = mybir.AxisListType

P = 128
C = 64
NH, HD = 8, 8
SIDE = 64
L = SIDE * SIDE
BATCH = 4
HALVES = 2
SLOTS = BATCH * L // P
QUADS = SLOTS // 4
CHUNKS = 8
WIN = 64
NS = 16
RANK = 16
NE, HID = 32, 16
BIG = 1e30
SCALE = float(HD) ** -0.5
LN_EPS = 1e-5
SCAN_EPS = 1e-12
TAIL = 64
BLK = 448
BLOCKS = (L - TAIL) // BLK
EXP_ZERO = -104.0

K_IDENT = 0
K_SWAP = K_IDENT + P
K_COSC = K_SWAP + P
K_SINC = K_COSC + 8
K_HEAD = K_SINC + 8
K_COSR = K_HEAD + NH
K_SINR = K_COSR + 32
K_REV = K_SINR + 32
K_SEG = K_REV + NE
K_EYE = K_SEG + 8 * TAIL
K_WIN = K_EYE + NE
K_END = K_WIN + 2


def vit_layer(nc, x, qkv_w, qkv_b, proj_w, proj_b, w_dbc, w_dt, b_dt, a_log, d_skip,
              router_w, router_b, w1, b1, w2, b2, consts, out):
    ctx = ExitStack()
    with ctx:
        def sb(name, shape, dt=F32):
            return ctx.enter_context(nc.sbuf_tensor(name, shape, dt))

        def sem(name):
            return ctx.enter_context(nc.semaphore(name))

        psum = ctx.enter_context(nc.psum_tensor("psum", [P, 8, 512], F32))
        banks = [psum[:, i, :] for i in range(8)]

        kc = sb("kc", [P, K_END])
        h_all = sb("h_all", [P, SLOTS, C])
        big_a = sb("big_a", [P, HALVES * L])
        big_b = sb("big_b", [P, HALVES * L])
        big_c = sb("big_c", [P, HALVES * L])
        u_all = sb("u_all", [P, HALVES * L])
        w_qkv_t = sb("w_qkv_t", [P, 3 * C])
        w_v = sb("w_v", [P, P])
        w_proj = sb("w_proj", [P, P])
        pb_row = sb("pb_row", [P, C])
        bv_col = sb("bv_col", [P, 1])

        ident = kc[:, K_IDENT:K_IDENT + P]
        xT, qT, kT = big_a, big_b, big_c

        def dup(eng, dst, src, s):
            for half in range(2):
                eng.dma_start(dst[64 * half:64 * half + 64], src).then_inc(s, 16)

        with ExitStack() as st1:
            def sb1(name, shape, dt=F32):
                return st1.enter_context(nc.sbuf_tensor(name, shape, dt))

            wraw = sb1("wraw", [P, 2, C])
            wraw2 = sb1("wraw2", [C, 2, C])
            praw = sb1("praw", [C, 2, C])
            w_swap = sb1("w_swap", [P, 2 * C])
            rot = sb1("rot", [P, 2, 2, 8, 2, 32])
            rtmp = sb1("rtmp", [P, 2, 8, 32])
            bqk = sb1("bqk", [P, 2])
            bqk_swap = sb1("bqk_swap", [P, 2])
            rbias = sb1("rbias", [P, 2, 8])
            rb_t = sb1("rb_t", [P, 8])

            kc_in, w_in, bqk_in, row_in = sem("kc_in"), sem("w_in"), sem("bqk_in"), sem("row_in")
            x_in = [sem(f"x_in{s}") for s in range(CHUNKS)]
            zeroed, wt_done, wt_copied = sem("zeroed"), sem("wt_done"), sem("wt_copied")
            prep, bias_ready, rot_ready = sem("prep"), sem("bias_ready"), sem("rot_ready")
            x_turned, x_left, x_right = sem("x_turned"), sem("x_left"), sem("x_right")
            qk_done, q_left, q_right = sem("qk_done"), sem("q_left"), sem("q_right")

            xin = h_all[:, :, :]

            def copy_x(eng, op, n, w, *kind):
                rho, j, c4 = n // 8, n // 2 % 4, n % 2
                eng.wait_ge(x_turned, 2 * n + w + 1)
                at = j * WIN + rho * 8 + c4 * 4
                a = xT[64 * w:64 * w + 64, at:at + 1]
                dst = bass.AP(tensor=a.tensor, offset=a.offset,
                              ap=[list(a.ap[0]), [1, 4], [4 * WIN, 32], [16, 4]])
                bank = banks[4 * w + n % 4]
                return op(dst, bank[0:64, :].rearrange("p (c a b) -> p c a b", c=4, a=32), *kind)

            with nc.Block() as block:
                @block.sync
                def _(sp):
                    sp.dma_start(kc[:, :], consts).then_inc(kc_in, 16)
                    rows = x.rearrange("b (a z) col d -> (b a) (z col) d", z=2)
                    for ch in range(CHUNKS):
                        sp.dma_start(xin[:, ch * 16:ch * 16 + 16, :], rows[:, ch * 16:ch * 16 + 16, :]
                                     ).then_inc(x_in[ch], 16)

                @block.scalar
                def _(act):
                    for d in range(2):
                        act.dma_start(wraw[:, d, :], qkv_w[0:2 * C, :]).then_inc(w_in, 16)
                        act.dma_start(wraw2[:, d, :], qkv_w[2 * C:3 * C, :]).then_inc(w_in, 16)
                        act.dma_start(praw[:, d, :], proj_w).then_inc(w_in, 16)
                    for qk in range(2):
                        for eta in range(2):
                            for w in range(2):
                                src = qkv_b[qk * C:qk * C + C].rearrange(
                                    "(h e d o) -> h e d o", e=2, d=4, o=1)[:, eta]
                                p0 = eta * 64 + w * 32
                                act.dma_start(bqk[p0:p0 + 32, qk:qk + 1], src).then_inc(bqk_in, 16)
                    act.dma_start(pb_row[:, :], proj_b.partition_broadcast(P)).then_inc(row_in, 16)
                    dup(act, bv_col, qkv_b[2 * C:3 * C].rearrange("(d o) -> d o", o=1), row_in)
                    act.preload_act_table_set("natural_log_exp_and_others")
                    for n in range(16):
                        copy_x(act, act.activation, n, 0, ACT.Copy).then_inc(x_left, 1)
                    for half in range(2):
                        if half == 0:
                            act.wait_ge(bias_ready, 1)
                        for n in range(16):
                            qk, v = n // 8, n % 8
                            dst = (qT, kT)[qk][0:64, half * L:half * L + L].rearrange(
                                "p (s r c) -> p s r c", r=8, c=8)[:, :, v, :]
                            act.wait_ge(qk_done, half * 16 + n + 1)
                            act.activation(dst, banks[4 + n % 4][0:64, :].rearrange("p (s c) -> p s c", c=8),
                                           ACT.Identity, bias=rbias[0:64, qk, v:v + 1],
                                           scale=SCALE if qk == 0 else 1.0).then_inc(q_left, 1)

                    act.wait_ge(row_in, 48)

                @block.gpsimd
                def _(pool):
                    pool.memset(rot[:, :, :, :, :, :], 0.0).then_inc(zeroed, 1)
                    pool.memset(w_v[:, :], 0.0).then_inc(zeroed, 1)
                    pool.memset(w_proj[:, :], 0.0).then_inc(zeroed, 1)

                @block.tensor
                def _(pe):
                    pe.wait_ge(kc_in, 16)
                    pe.wait_ge(w_in, 16 * 6)
                    pe.transpose(banks[2][:, 0:P], wraw[:, :, :], ident)
                    pe.transpose(banks[2][:, P:P + C], wraw2[:, :, :], kc[0:C, 0:C])
                    pe.transpose(banks[2][:, P + C:2 * P], praw[:, :, :], kc[0:C, 0:C]).then_inc(wt_done, 1)
                    pe.wait_ge(bqk_in, 16 * 8)
                    pe.matmul(banks[3][:, 0:2], kc[:, K_SWAP:K_SWAP + P], bqk[:, :],
                              start=True, stop=True).then_inc(wt_done, 1)
                    pe.wait_ge(prep, 3)
                    for n in range(16):
                        rho, j, c4 = n // 8, n // 2 % 4, n % 2
                        pe.wait_ge(x_in[rho * 4 + j], 16)
                        for w in range(2):
                            if n >= 4:
                                pe.wait_ge((x_left, x_right)[w], n - 3)
                            for c in range(4):
                                t0 = rho * SIDE + j * 16 + w * 8 + c4 * 4 + c
                                t = pe.transpose(banks[4 * w + n % 4][0:64, c * P:c * P + P], xin[:, t0, :], ident)
                            t.then_inc(x_turned, 1)
                    pe.wait_ge(x_left, 16)
                    pe.wait_ge(x_right, 16)
                    for half in range(2):
                        pe.wait_ge(rot_ready, 4)
                        xh = xT[:, half * L:half * L + L].rearrange("p (s r c) -> p s r c", r=8, c=8)
                        for n in range(16):
                            qk, v = n // 8, n % 8
                            m = half * 16 + n
                            if m >= 4:
                                pe.wait_ge(q_left, m - 3)
                                pe.wait_ge(q_right, m - 3)
                            bank = banks[4 + n % 4]
                            pe.matmul(bank[0:64, :], rot[:, qk, 0, v], xh[:, :, v, :],
                                      start=True, stop=True)
                            pe.matmul(bank[64:128, :], rot[:, qk, 1, v], xh[:, :, :, v],
                                      start=True, stop=True).then_inc(qk_done, 1)

                @block.vector
                def _(dve):
                    dve.wait_ge(zeroed, 3)
                    dve.wait_ge(wt_done, 1)
                    dve.tensor_copy(w_qkv_t[:, :], banks[2][:, 0:3 * C]).then_inc(wt_copied, 1)
                    for w in range(2):
                        q = slice(64 * w, 64 * w + 64)
                        dve.tensor_copy(w_proj[q, q], banks[2][q, 3 * C:4 * C]).then_inc(wt_copied, 1)
                    dve.wait_ge(wt_copied, 3)
                    for w in range(2):
                        q = slice(64 * w, 64 * w + 64)
                        dve.tensor_copy(w_v[q, q], w_qkv_t[q, 2 * C:3 * C])
                    pairs = w_qkv_t[:, 0:2 * C].rearrange("p (n e) -> p n e", e=2)
                    swaps = w_swap[:, :].rearrange("p (n e) -> p n e", e=2)
                    dve.tensor_copy(swaps[:, :, 0], pairs[:, :, 1]).then_inc(prep, 1)
                    dve.tensor_copy(swaps[:, :, 1], pairs[:, :, 0]).then_inc(prep, 1)
                    dve.wait_ge(wt_done, 2)
                    dve.tensor_copy(bqk_swap[:, :], banks[3][:, 0:2]).then_inc(prep, 1)
                    dve.wait_ge(prep, 3)
                    done = 3
                    for qk in range(2):
                        for eta in range(2):
                            def part(src):
                                v = src[:, qk * C:qk * C + C].rearrange("p (h e d) -> p h e d", e=2, d=4)
                                return v[:, :, eta, :].unsqueeze(1).broadcast_to([P, 8, 8, 4])

                            def trig(at):
                                v = kc[:, at:at + 32].rearrange("p (v d) -> p v d", d=4)
                                return v.unsqueeze(2).broadcast_to([P, 8, 8, 4])

                            dst = [rtmp[:, i].rearrange("p v (h d) -> p v h d", d=4) for i in range(2)]
                            dve.tensor_tensor(dst[0], part(w_qkv_t), trig(K_COSR), ALU.mult).then_inc(prep, 1)
                            dve.tensor_tensor(dst[1], part(w_swap), trig(K_SINR), ALU.mult).then_inc(prep, 1)
                            done += 2
                            dve.wait_ge(prep, done)
                            for w in range(2):
                                q = slice(64 * w, 64 * w + 64)
                                i = dve.tensor_tensor(rot[q, qk, eta, :, w, :], rtmp[q, 0], rtmp[q, 1], ALU.add)
                                i.then_inc(prep, 1)
                            done += 2
                            dve.wait_ge(prep, done)
                            dve.sem_inc(rot_ready, 1)
                    for qk in range(2):
                        dve.tensor_scalar(rb_t[:, :], kc[:, K_COSC:K_COSC + 8], bqk[:, qk:qk + 1],
                                          SCALE if qk == 0 else 1.0, ALU.mult, ALU.mult).then_inc(prep, 1)
                        dve.tensor_scalar(rbias[:, qk, :], kc[:, K_SINC:K_SINC + 8], bqk_swap[:, qk:qk + 1],
                                          SCALE if qk == 0 else 1.0, ALU.mult, ALU.mult).then_inc(prep, 1)
                        done += 2
                        dve.wait_ge(prep, done)
                        dve.tensor_tensor(rbias[:, qk, :], rbias[:, qk, :], rb_t[:, :], ALU.add).then_inc(prep, 1)
                        done += 1
                        dve.wait_ge(prep, done)
                    dve.sem_inc(bias_ready, 1)
                    for n in range(16):
                        copy_x(dve, dve.tensor_copy, n, 1).then_inc(x_right, 1)
                    for half in range(2):
                        for n in range(16):
                            qk, v = n // 8, n % 8
                            dst = (qT, kT)[qk][64:128, half * L:half * L + L].rearrange(
                                "p (s r c) -> p s r c", r=8, c=8)[:, :, :, v]
                            dve.wait_ge(qk_done, half * 16 + n + 1)
                            src = banks[4 + n % 4][64:128, :].rearrange("p (s c) -> p s c", c=8)
                            dve.tensor_scalar(dst, src, SCALE if qk == 0 else 1.0, rbias[64:128, qk, v:v + 1],
                                              ALU.mult, ALU.add).then_inc(q_right, 1)

        attention(nc, dict(kc=kc, h_all=h_all, xT=xT, qT=qT, kT=kT, w_v=w_v, w_proj=w_proj,
                           pb_row=pb_row, bv_col=bv_col, banks=banks, u_all=u_all))

        selective_scan(nc, dict(kc=kc, psum=psum, u=u_all, y=big_b, du=big_a, later=big_c, spare=(w_v, w_proj)),
                       w_dbc, w_dt, b_dt, a_log, d_skip, h_all,
                       (router_w, router_b, w1, b1, w2, b2), out)


def attention(nc, t):
    kc, h_all, xT, qT, kT, u_all, banks = (t[n] for n in ("kc", "h_all", "xT", "qT", "kT", "u_all", "banks"))
    w_v, w_proj, pb_row, bv_col = (t[n] for n in ("w_v", "w_proj", "pb_row", "bv_col"))
    ident = kc[:, K_IDENT:K_IDENT + P]
    with ExitStack() as ctx:
        def sb(name, shape, dt=F32):
            return ctx.enter_context(nc.sbuf_tensor(name, shape, dt))

        def sem(name):
            return ctx.enter_context(nc.semaphore(name))

        q_st = sb("q_st", [P, 4, 2, WIN])
        k_st = sb("k_st", [P, 4, NH, WIN])
        x_st = sb("x_st", [P, 4, 2, WIN])
        top = sb("top", [P, 2, NH])
        low = sb("low", [P, 2, NH, WIN])
        prob = sb("prob", [P, 2, NH * WIN])
        prob_t = sb("prob_t", [P, 2, 512])
        v_st = sb("v_st", [P, 4, 2, 4, 2, HD + 1])
        inv = sb("inv", [P, 2, 2 * 4 * 2])
        o_st = sb("o_st", [P, 4, C])
        o_t = sb("o_t", [P, 2, P])
        nsum = sb("nsum", [P, 4])
        xc = sb("xc", [P, 4, C])
        sq = sb("sq", [P, 4, C])
        ssum = sb("ssum", [P, 4])
        var = sb("var", [P, 4])
        mhalf = sb("mhalf", [P, 4])
        rstd = sb("rstd", [P, 4])
        xh = sb("xh", [P, 4, C])

        q_masked, power_set, v_zeroed, ones_set = sem("q_masked"), sem("power_set"), sem("v_zeroed"), sem("ones_set")
        x_staged, k_masked, scores_done = sem("x_staged"), sem("k_masked"), sem("scores_done")
        top_done, low_done, prob_done = sem("top_done"), sem("low_done"), sem("prob_done")
        turned, prob_t_done, pv_done = sem("turned"), sem("prob_t_done"), sem("pv_done")
        v_done, v_copied = sem("v_done"), sem("v_copied")
        inv_done, o_done, ot_done, ot_copied = sem("inv_done"), sem("o_done"), sem("ot_done"), sem("ot_copied")
        proj_done, h_done, nsum_done, xc_done = sem("proj_done"), sem("h_done"), sem("nsum_done"), sem("xc_done")
        sq_done, ssum_done, var_done = sem("sq_done"), sem("ssum_done"), sem("var_done")
        rstd_done, xh_done = sem("rstd_done"), sem("xh_done")
        u_turned, u_copied = sem("u_turned"), sem("u_copied")

        LAST = QUADS + 4

        def steps(eng, body):
            for i in range(4):
                body(i)
            with eng.Fori(4, QUADS) as i:
                body(i)
            for i in range(QUADS, LAST + 1):
                body(i)

        def live(i, lag):
            return not isinstance(i, int) or 0 <= i - lag < QUADS

        def first(i, lag=0):
            return isinstance(i, int) and i - lag <= 0

        with nc.Block() as block:
            @block.sync
            def _(sp):
                def body(i):
                    if not first(i):
                        sp.wait_ge(v_done, i)
                    for d in range(2):
                        for k in range(2):
                            sp.dma_start(x_st[:, 2 * k:2 * k + 2, d, :], slot_pair(xT, i, k)).then_inc(x_staged, 16)

                body(0)
                with sp.Fori(1, QUADS) as i:
                    body(i)

            @block.gpsimd
            def _(pool):
                pool.memset(mhalf[:, :], -0.5).then_inc(power_set, 1)
                pool.wait_ge(power_set, 1)
                mask = kc[:, K_HEAD:K_HEAD + NH].unsqueeze(2).broadcast_to([P, NH, WIN])

                of_window = kc[:, K_WIN:K_WIN + 2].unsqueeze(1).unsqueeze(3).broadcast_to([P, 2, 2, WIN])

                def mask_q(i, k):
                    if not first(i):
                        pool.wait_ge(scores_done, i * 4 + (2 * k - 2))
                    q = slot_pair(qT, i, k).unsqueeze(2).broadcast_to([P, 2, 2, WIN])
                    pool.tensor_tensor(q_st[:, 2 * k:2 * k + 2], q, of_window, ALU.mult).then_inc(q_masked, 1)

                def mask_k(i, s):
                    if not first(i):
                        pool.wait_ge(scores_done, i * 4 + (s - 3))
                    k = slot_pair(kT, i, s // 2)[:, s % 2, :].unsqueeze(1).broadcast_to([P, NH, WIN])
                    pool.tensor_tensor(k_st[:, s], k, mask, ALU.mult).then_inc(k_masked, 1)

                def body(i):
                    if live(i, 0):
                        mask_k(i, 0)
                        mask_q(i, 0)
                        mask_k(i, 1)
                    if live(i, 3):
                        pool.wait_ge(xc_done, i - 2)
                        pool.tensor_tensor(sq[:, :, :], xc[:, :, :], xc[:, :, :], ALU.mult).then_inc(sq_done, 1)
                    if live(i, 0):
                        mask_k(i, 2)
                        mask_q(i, 1)
                    if live(i, 3):
                        pool.wait_ge(var_done, i - 2)
                        pool.tensor_tensor(rstd[:, :], var[:, :], mhalf[:, :], ALU.pow).then_inc(rstd_done, 1)
                        pool.wait_ge(rstd_done, i - 2)
                        pool.wait_ge(u_turned, i - 3)
                        pool.tensor_tensor(xh[:, :, :], xc[:, :, :],
                                           rstd[:, :].unsqueeze(2).broadcast_to([P, 4, C]), ALU.mult
                                           ).then_inc(xh_done, 1)
                    if live(i, 0):
                        mask_k(i, 3)

                steps(pool, body)

            @block.tensor
            def _(pe):
                pe.wait_ge(ones_set, 2)

                def scores(i, s):
                    pe.wait_ge(k_masked, i * 4 + (s + 1))
                    pe.wait_ge(q_masked, i * 2 + (s // 2 + 1))
                    if not (first(i) and s < 2):
                        pe.wait_ge(low_done, i * 4 + (s - 1))
                    pe.matmul(banks[s % 2][:, :], q_st[:, s], k_st[:, s], start=True, stop=True
                              ).then_inc(scores_done, 1)

                def turn(i, s):
                    pe.wait_ge(prob_done, i * 4 + (s + 1))
                    if not (first(i) and s < 2):
                        pe.wait_ge(prob_t_done, i * 4 + (s - 1))
                    for n in range(4):
                        m = pe.transpose(banks[2 + s % 2][:, n * P:n * P + P],
                                         prob[:, s % 2, n * P:n * P + P], ident)
                    m.then_inc(turned, 1)

                def products(i, s):
                    pe.wait_ge(prob_t_done, i * 4 + (s + 1))
                    pe.wait_ge(v_copied, i * 2 + (s // 2 + 1))
                    if s % 2 == 0 and not first(i):
                        pe.wait_ge(o_done, i * 2 + (s // 2 - 1))
                    o = banks[4 + s // 2][:, (s % 2) * 144:(s % 2) * 144 + 144]
                    for n in range(4):
                        m = pe.matmul(o[:, n * 36:n * 36 + 36], prob_t[:, s % 2, n * P:n * P + P],
                                      v_st[:, s, :, n, :, :], start=(s % 2 == 0 and n == 0), stop=True,
                                      skip_group_check=True)
                    m.then_inc(pv_done, 1)

                def body(i):
                    if live(i, 0):
                        scores(i, 0)
                    if live(i, 1):
                        turn(i - 1, 2)
                        products(i - 1, 1)
                    if live(i, 2):
                        pe.wait_ge(o_done, i * 2 - 2)
                        if not first(i, 2):
                            pe.wait_ge(h_done, i - 2)
                        for n in range(2):
                            m = pe.transpose(banks[7][:, n * P:n * P + P], o_st[:, 2 * n:2 * n + 2, :], ident)
                        m.then_inc(ot_done, 1)
                    if live(i, 0):
                        pe.wait_ge(x_staged, (i + 1) * 64)
                        if not first(i):
                            pe.wait_ge(v_copied, i * 2)
                        for s in range(4):
                            m = pe.matmul(banks[6][:, s * P:s * P + P], x_st[:, s], w_v[:, :],
                                          start=True, stop=True, skip_group_check=True)
                        m.then_inc(v_done, 1)
                        scores(i, 1)
                    if live(i, 1):
                        turn(i - 1, 3)
                        products(i - 1, 2)
                    if live(i, 4):
                        pe.wait_ge(xh_done, i - 3)
                        if live(i, 2):
                            pe.wait_ge(ot_copied, i - 1)
                        else:
                            pe.wait_ge(h_done, QUADS)
                            pe.wait_ge(u_copied, i - 4)
                        for n in range(2):
                            m = pe.transpose(banks[7][:, n * P:n * P + P], xh[:, 2 * n:2 * n + 2, :], ident)
                        m.then_inc(u_turned, 1)
                    if live(i, 0):
                        scores(i, 2)
                        turn(i, 0)
                    if live(i, 1):
                        products(i - 1, 3)
                    if live(i, 0):
                        scores(i, 3)
                        turn(i, 1)
                        products(i, 0)
                    if live(i, 2):
                        pe.wait_ge(ot_copied, i - 1)
                        if live(i, 4):
                            pe.wait_ge(u_copied, i - 3)
                        for n in range(2):
                            m = pe.matmul(banks[7][:, 256 + n * P:256 + n * P + P], o_t[:, n, :], w_proj[:, :],
                                          start=(n == 0), stop=True, skip_group_check=True)
                        m.then_inc(proj_done, 1)

                steps(pe, body)

            @block.scalar
            def _(act):
                act.wait_ge(ones_set, 2)

                def exps(i, s):
                    act.wait_ge(low_done, i * 4 + (s + 1))
                    if not (first(i) and s < 2):
                        act.wait_ge(turned, i * 4 + (s - 1))
                    act.activation(prob[:, s % 2, :], low[:, s % 2], ACT.Exp).then_inc(prob_done, 1)

                def copy_t(i, s):
                    act.wait_ge(turned, i * 4 + (s + 1))
                    if not (first(i) and s < 2):
                        act.wait_ge(pv_done, i * 4 + (s - 1))
                    act.activation(prob_t[:, s % 2, :], banks[2 + s % 2][:, :], ACT.Copy).then_inc(prob_t_done, 1)

                def copy_v(i, hf):
                    act.wait_ge(v_done, i + 1)
                    if not first(i):
                        act.wait_ge(pv_done, i * 4 + (2 * hf - 2))
                    for e in range(2):
                        q = slice(64 * e, 64 * e + 64)
                        src = banks[6][q, hf * 256:hf * 256 + 256].rearrange(
                            "p (sw n e d) -> p sw n e d", n=4, e=2, d=HD)[:, :, :, e, :]
                        dst = v_st[q, 2 * hf:2 * hf + 2, :, :, e, 0:HD].rearrange("p s w n d -> p (s w) n d")
                        a = act.activation(dst, src, ACT.Copy)
                    a.then_inc(v_copied, 1)

                def body(i):
                    if live(i, 1):
                        copy_t(i - 1, 2)
                    if live(i, 0):
                        exps(i, 0)
                    if live(i, 2):
                        act.wait_ge(ot_done, i - 1)
                        if not first(i, 2):
                            act.wait_ge(proj_done, i - 2)
                        for n in range(2):
                            a = act.activation(o_t[:, n, :].rearrange("p (r w c) -> p w r c", w=2, r=8),
                                               banks[7][:, n * P:n * P + P].rearrange("p (w r c) -> p w r c", w=2, r=8),
                                               ACT.Identity, bias=bv_col[:, 0:1])
                        a.then_inc(ot_copied, 1)
                    if live(i, 1):
                        copy_t(i - 1, 3)
                    if live(i, 0):
                        copy_v(i, 0)
                        exps(i, 1)
                    if live(i, 4):
                        act.wait_ge(u_turned, i - 3)
                        j = i - 4
                        at = j // 2 * 512 + j % 2 * 32
                        a = act.activation(raster(u_all, at), banks[7][:, 0:256].rearrange(
                            "p (k r x) -> p k r x", k=2, r=8), ACT.Copy)
                        a.then_inc(u_copied, 1)
                    if live(i, 0):
                        copy_t(i, 0)
                        exps(i, 2)
                        copy_t(i, 1)
                        exps(i, 3)
                        copy_v(i, 1)

                steps(act, body)

            @block.vector
            def _(dve):
                ones = v_st[:, :, :, :, :, HD]
                dve.memset(v_st[:, :, :, :, :, :], 0.0).then_inc(v_zeroed, 1)
                dve.wait_ge(v_zeroed, 1)
                for e in range(2):
                    q = slice(64 * e, 64 * e + 64)
                    dve.memset(v_st[q, :, :, :, e, HD:HD + 1].rearrange("p s w n o -> p (s w) n o"), 1.0
                               ).then_inc(ones_set, 1)

                def lower(i, s):
                    sc = banks[s % 2][:, :].rearrange("p (h k) -> p h k", h=NH)
                    dve.wait_ge(scores_done, i * 4 + (s + 1))
                    dve.tensor_reduce(top[:, s % 2, :], sc, AX.X, ALU.max).then_inc(top_done, 1)
                    dve.wait_ge(top_done, i * 4 + (s + 1))
                    if not (first(i) and s < 2):
                        dve.wait_ge(prob_done, i * 4 + (s - 1))
                    dve.tensor_tensor(low[:, s % 2], sc,
                                      top[:, s % 2, :].unsqueeze(2).broadcast_to([P, NH, WIN]),
                                      ALU.subtract).then_inc(low_done, 1)

                def normalise(i, hf):
                    dve.wait_ge(pv_done, i * 4 + (2 * hf + 2))
                    if not first(i):
                        dve.wait_ge(ot_done, i)
                    o = banks[4 + hf][:, 0:288].rearrange("p (sn w e d) -> p sn w e d", sn=8, w=2, e=2)
                    for w in range(2):
                        q = slice(64 * w, 64 * w + 64)
                        dve.reciprocal(inv[q, hf, :].rearrange("p (sn e) -> p sn e", e=2),
                                       o[q, :, w, :, HD]).then_inc(inv_done, 1)
                    dve.wait_ge(inv_done, i * 4 + (2 * hf + 2))
                    for w in range(2):
                        q = slice(64 * w, 64 * w + 64)
                        m = dve.tensor_tensor(
                            o_st[q, 2 * hf:2 * hf + 2, :].rearrange("p s (n e d) -> p (s n) e d", n=4, e=2),
                            o[q, :, w, :, 0:HD],
                            inv[q, hf, :].rearrange("p (sn e) -> p sn e", e=2).unsqueeze(3).broadcast_to([64, 8, 2, HD]),
                            ALU.mult)
                    m.then_inc(o_done, 1)

                def body(i):
                    if live(i, 0):
                        lower(i, 0)
                    if live(i, 3):
                        h = h_all[:, bass.ds(i * 4 - 12, 4), :]
                        dve.tensor_reduce(nsum[:, :], h, AX.X, ALU.add, negate=True).then_inc(nsum_done, 1)
                        dve.wait_ge(nsum_done, i - 2)
                        if not first(i, 3):
                            dve.wait_ge(xh_done, i - 3)
                        dve.scalar_tensor_tensor(xc[:, :, :], nsum[:, :].unsqueeze(2).broadcast_to([P, 4, C]),
                                                 1.0 / C, h, ALU.mult, ALU.add).then_inc(xc_done, 1)
                    if live(i, 0):
                        lower(i, 1)
                    if live(i, 1):
                        normalise(i - 1, 0)
                    if live(i, 0):
                        lower(i, 2)
                    if live(i, 3):
                        dve.wait_ge(sq_done, i - 2)
                        dve.tensor_reduce(ssum[:, :], sq[:, :, :], AX.X, ALU.add).then_inc(ssum_done, 1)
                        dve.wait_ge(ssum_done, i - 2)
                        dve.tensor_scalar(var[:, :], ssum[:, :], 1.0 / C, LN_EPS, ALU.mult, ALU.add
                                          ).then_inc(var_done, 1)
                    if live(i, 0):
                        lower(i, 3)
                    if live(i, 1):
                        normalise(i - 1, 1)
                    if live(i, 2):
                        dve.wait_ge(proj_done, i - 1)
                        dve.tensor_tensor(h_all[:, bass.ds(i * 4 - 8, 4), :],
                                          banks[7][:, 256:512].rearrange("p (s d) -> p s d", s=4),
                                          pb_row[:, :].unsqueeze(1).broadcast_to([P, 4, C]), ALU.add
                                          ).then_inc(h_done, 1)
                        dve.wait_ge(h_done, i - 1)

                steps(dve, body)


def slot_pair(arr, i, k):
    a = arr[:, bass.ds(i * (2 * WIN) + i // 16 * (L // 2) + k * WIN, L // 2 + WIN)]
    return bass.AP(tensor=a.tensor, offset=a.offset, ap=[list(a.ap[0]), [L // 2, 2], [1, WIN]],
                   dep_tracking_offset=a.dep_tracking_offset)


def raster(arr, at):
    a = arr[:, bass.ds(at, 7 * SIDE + 32)]
    return bass.AP(tensor=a.tensor, offset=a.offset, ap=[list(a.ap[0]), [16, 2], [SIDE, 8], [1, 16]],
                   dep_tracking_offset=a.dep_tracking_offset)


def selective_scan(nc, t, w_dbc, w_dt, b_dt, a_log, d_skip, h_all, moe, out):
    kc, psum, u, y, du, later = (t[n] for n in ("kc", "psum", "u", "y", "du", "later"))
    ident = kc[:, K_IDENT:K_IDENT + P]
    with ExitStack() as ctx:
        with ExitStack() as scan_ctx:
            scan_stages(nc, scan_ctx, kc, psum, u, du, later, y, ident,
                        w_dbc, w_dt, b_dt, a_log, d_skip, t["spare"])
        experts(nc, ctx, kc, psum, y, h_all, ident, moe, out)


def scan_stages(nc, ctx, kc, psum, u, du, later, y, ident, w_dbc, w_dt, b_dt, a_log, d_skip, spare):
    def sb(name, shape, dt=F32):
        return ctx.enter_context(nc.sbuf_tensor(name, shape, dt))

    def sem(name):
        return ctx.enter_context(nc.semaphore(name))

    wd = sb("wd", [P, RANK + 2 * NS])
    wdt = sb("wdt", [RANK, C])
    wd_t = sb("wd_t", [RANK, P])
    w_delta = sb("w_delta", [P, P])
    w_rep = sb("w_rep", [P, 2 * NS, P])
    b_col = sb("b_col", [P, 1])
    d_col = sb("d_col", [P, 1])
    a_neg = sb("a_neg", [P, NS])
    ones = sb("ones", [P, 1])
    eps = sb("eps", [P, 1])
    rmin = sb("rmin", [P, 2])
    alive = sb("alive", [P, 2 * NS])
    alive_n = sb("alive_n", [1, 2 * NS], I32)
    carry = sb("carry", [P, HALVES, NS])
    buf_a = sb("buf_a", [P, NS * P])
    buf_b = sb("buf_b", [P, NS * P])
    buf_c = sb("buf_c", [P, NS * P])
    mag = buf_a[:, 0:1024].rearrange("p (a b) -> p a b", a=2)

    small_in, rep_zeroed, const_set = sem("small_in"), sem("rep_zeroed"), sem("const_set")
    wt_turned, wt_copied, wd_done, wd_copied = sem("wdt_turned"), sem("wdt_copied"), sem("wd_done"), sem("wd_copied")
    rep_done, a_done, z_done, z_read = sem("rep_done"), sem("a_done"), sem("z_done"), sem("z_read")
    e_done, ln_done, delta_done, scan_done = sem("e_done"), sem("ln_done"), sem("delta_done"), sem("scan_done")
    pos_done = sem("pos_done")
    last_set, y_set, du_done = sem("last_set"), sem("y_set"), sem("du_done")
    rmin_done, alive_done, count_done, flag_done = sem("rmin_done"), sem("alive_done"), sem("count_done"), sem("flag_done")
    CH = HALVES * L // 512

    with nc.Block() as block:
        @block.sync
        def _(sp):
            for b in range(2):
                q = slice(64 * b, 64 * b + 64)
                sp.dma_start(wd[q], w_dbc).then_inc(small_in, 16)
                sp.dma_start(b_col[q], b_dt.rearrange("(d o) -> d o", o=1)).then_inc(small_in, 16)
                sp.dma_start(d_col[q], d_skip.rearrange("(d o) -> d o", o=1)).then_inc(small_in, 16)
                sp.dma_start(a_neg[q], a_log).then_inc(small_in, 16)
            sp.dma_start(wdt[:, :], w_dt).then_inc(small_in, 16)
            sp.wait_ge(small_in, 16 * 9)

        @block.tensor
        def _(pe):
            pe.wait_ge(small_in, 16 * 9)
            pe.transpose(psum[0:RANK, 7, 0:P], wd[:, 0:RANK], ident).then_inc(wt_turned, 1)
            pe.wait_ge(wt_copied, 1)
            pe.matmul(psum[:, 7, 0:C], wd_t[:, :], wdt[:, :], start=True, stop=True).then_inc(wd_done, 1)
            pe.wait_ge(wd_copied, 2)
            for n in range(CH):
                if n >= 4:
                    pe.wait_ge(z_read, n - 3)
                pe.matmul(psum[:, n % 4, :], w_delta[:, :], u[:, n * 512:n * 512 + 512],
                          start=True, stop=True).then_inc(z_done, 1)
            pe.wait_ge(const_set, 2)
            pe.wait_ge(alive_done, 2)
            pe.matmul(psum[0:1, 7, 0:2 * NS], ones[:, :], alive[:, :], start=True, stop=True).then_inc(count_done, 1)

        @block.vector
        def _(dve):
            dve.memset(w_delta[:, :], 0.0).then_inc(rep_zeroed, 1)
            dve.wait_ge(wt_turned, 1)
            dve.tensor_copy(wd_t[:, :], psum[0:RANK, 7, 0:P]).then_inc(wt_copied, 1)
            dve.wait_ge(wd_done, 1)
            dve.wait_ge(rep_zeroed, 1)
            for b in range(2):
                q = slice(64 * b, 64 * b + 64)
                dve.tensor_copy(w_delta[q, q], psum[q, 7, 0:C]).then_inc(wd_copied, 1)
            dve.wait_ge(a_done, 1)
            dve.tensor_scalar(a_neg[:, :], a_neg[:, :], -1.0, None, ALU.mult).then_inc(a_done, 1)
            for n in range(CH):
                dve.wait_ge(z_done, n + 1)
                dve.tensor_scalar(du[:, n * 512:n * 512 + 512], psum[:, n % 4, :], b_col[:, 0:1], 0.0,
                                  ALU.add, ALU.max).then_inc(pos_done, 1)
                dve.wait_ge(pos_done, n + 1)
                if n >= 2:
                    dve.wait_ge(e_done, n - 1)
                dve.scalar_tensor_tensor(mag[:, n % 2, :], du[:, n * 512:n * 512 + 512], -2.0, psum[:, n % 4, :],
                                         ALU.mult, ALU.add).then_inc(z_read, 1)
            dve.wait_ge(const_set, 2)
            dve.wait_ge(last_set, 2)
            for half in range(HALVES):
                dve.wait_ge(delta_done, (half + 1) * CH // 2)
                at = half * L
                dve.tensor_tensor_scan(backwards(later, at, L - 1, P), ones[:, 0:1].to_broadcast([P, L - 1]),
                                       backwards(du, at + 1, L - 1, P), 0.0, ALU.mult, ALU.add
                                       ).then_inc(scan_done, 1)
            dve.wait_ge(scan_done, 2)
            for m, last in enumerate((L - TAIL - BLK - 1, L - TAIL - 1)):
                dve.tensor_tensor(rmin[:, m:m + 1], later[:, last:last + 1], later[:, L + last:L + last + 1],
                                  ALU.min).then_inc(rmin_done, 1)
            dve.wait_ge(rmin_done, 2)
            dve.wait_ge(a_done, 2)
            for m in range(2):
                dve.tensor_scalar(alive[:, m * NS:m * NS + NS], a_neg[:, :], rmin[:, m:m + 1], EXP_ZERO,
                                  ALU.mult, ALU.is_gt).then_inc(alive_done, 1)
            at = L
            dve.tensor_tensor(du[:, at:at + L], du[:, at:at + L], u[:, at:at + L], ALU.mult).then_inc(du_done, 1)
            dve.wait_ge(count_done, 1)
            dve.tensor_copy(alive_n[:, :], psum[0:1, 7, 0:2 * NS]).then_inc(flag_done, 1)

        @block.scalar
        def _(act):
            act.wait_ge(small_in, 16 * 9)
            act.activation(a_neg[:, :], a_neg[:, :], ACT.Exp).then_inc(a_done, 1)
            act.wait_ge(const_set, 2)
            for b in range(2):
                q = slice(64 * b, 64 * b + 64)
                act.activation(w_rep[q, :, q], wd[q, RANK:].unsqueeze(2).to_broadcast([64, 2 * NS, 64]), ACT.Copy)
            for n in range(CH):
                act.wait_ge(z_read, n + 1)
                m = slice(n * 512, n * 512 + 512)
                act.activation(later[:, m], mag[:, n % 2, :], ACT.Exp, bias=b_col[:, 0:1]).then_inc(e_done, 1)
                act.wait_ge(e_done, n + 1)
                act.activation(later[:, m], later[:, m], ACT.Ln, bias=1.0).then_inc(ln_done, 1)
            for n in range(4):
                m = slice(n * 2048, n * 2048 + 2048)
                act.activation(y[:, m], u[:, m], ACT.Copy, scale=d_col[:, 0:1]).then_inc(y_set, 1)

        @block.gpsimd
        def _(pool):
            pool.memset(w_rep[:, :, :], 0.0).then_inc(const_set, 1)
            pool.memset(ones[:, :], 1.0).then_inc(const_set, 1)
            pool.memset(eps[:, :], SCAN_EPS)
            pool.memset(carry[:, :, :], 0.0)
            for n in range(CH):
                pool.wait_ge(ln_done, n + 1)
                m = slice(n * 512, n * 512 + 512)
                pool.tensor_tensor(du[:, m], du[:, m], later[:, m], ALU.add).then_inc(delta_done, 1)
            pool.wait_ge(delta_done, CH)
            for half in range(HALVES):
                pool.memset(later[:, half * L + L - 1:half * L + L], 0.0).then_inc(last_set, 1)
            pool.wait_ge(scan_done, 1)
            pool.tensor_tensor(du[:, 0:L], du[:, 0:L], u[:, 0:L], ALU.mult).then_inc(du_done, 1)

    rep_staged, bc_done, cum_done, lnc_done, rec_done = (
        sem("rep_staged"), sem("bc_done"), sem("cum_done"), sem("lnc_done"), sem("rec_done"))
    duc_done, term_done, sum_done, ratio_done, out_done, y_added, carried = (
        sem("duc_done"), sem("term_done"), sem("sum_done"), sem("ratio_done"), sem("out_done"),
        sem("y_added"), sem("carried"))
    state_set, state_kept = sem("state_set"), sem("state_kept")
    w_b, w_c = spare
    a_n = sb("a_n", [P, 1])
    state = sb("state", [P, HALVES])

    def two(buf, r):
        return buf[:, r * 2 * BLK:(r + 1) * 2 * BLK].rearrange("p (a t) -> p a t", a=2)

    def block_of(arr, blk):
        if isinstance(blk, int):
            return arr[:, :].rearrange("p (a t) -> p a t", a=2)[:, :, blk * BLK:blk * BLK + BLK]
        return arr[:, :].rearrange("p (a t) -> p a t", a=2)[:, :, bass.ds(blk * BLK, BLK)]

    def blocks(eng, load, n, body, skip):
        far = load(alive_n[0:1, bass.ds(n, 1)], min_val=0, max_val=P)
        near = load(alive_n[0:1, bass.ds(n + NS, 1)], min_val=0, max_val=P)
        with eng.If(far > 0):
            with eng.Fori(0, (BLOCKS - 1) // 2) as pair:
                for r in range(2):
                    body(n * BLOCKS + pair * 2 + r, pair * 2 + r, r)
        with eng.Else():
            skip(BLOCKS - 1)
        with eng.If(near > 0):
            body(n * BLOCKS + (BLOCKS - 1), BLOCKS - 1, 0)
        with eng.Else():
            skip(1)

    with nc.Block() as block:
        @block.gpsimd
        def _(pool):
            def body(q, blk, r):
                pool.wait_ge(lnc_done, q + 1)
                pool.tensor_tensor(two(buf_a, r), two(buf_a, r), block_of(du, blk), ALU.mult).then_inc(duc_done, 1)
                pool.wait_ge(out_done, q + 1)
                pool.tensor_tensor(block_of(y, blk), block_of(y, blk), two(buf_c, r), ALU.add).then_inc(y_added, 1)

            def skip(n):
                pool.sem_inc(duc_done, n)
                pool.sem_inc(y_added, n)

            with pool.Fori(0, NS) as n:
                pool.wait_ge(bc_done, n * BLOCKS)
                pool.wait_ge(cum_done, n * BLOCKS)
                pool.tensor_copy(w_b[:, :], w_rep[:, bass.ds(n, 1), :].rearrange("p o d -> p (o d)")).then_inc(rep_staged, 1)
                pool.tensor_copy(w_c[:, :], w_rep[:, bass.ds(n + NS, 1), :].rearrange("p o d -> p (o d)")).then_inc(rep_staged, 1)
                pool.tensor_copy(a_n[:, :], a_neg[:, bass.ds(n, 1)]).then_inc(rep_staged, 1)
                blocks(pool, pool.value_load, n, body, skip)

        @block.tensor
        def _(pe):
            def body(q, blk, r):
                pe.wait_ge(out_done, q)
                for k, w in enumerate((w_b, w_c)):
                    for half in range(HALVES):
                        m = pe.matmul(psum[:, 4 * r + 2 * k + half, 0:BLK], w[:, :],
                                      u[:, bass.ds(half * L + blk * BLK, BLK)], start=True, stop=True)
                m.then_inc(bc_done, 1)

            def skip(n):
                pe.sem_inc(bc_done, n)

            with pe.Fori(0, NS) as n:
                pe.wait_ge(rep_staged, n * 3 + 3)
                blocks(pe, pe.value_load, n, body, skip)
            pe.wait_ge(out_done, NS * BLOCKS)
            tail = u[:, :].rearrange("p (a t) -> p a t", a=2)[:, :, L - TAIL:L]
            for n in range(2 * NS):
                m = pe.matmul(psum[:, n // 4, n % 4 * P:n % 4 * P + P], w_rep[:, n, :], tail,
                              start=True, stop=True, skip_group_check=True)
                if n % NS == NS - 1:
                    m.then_inc(bc_done, 1)

        @block.scalar
        def _(act):
            def body(q, blk, r):
                act.wait_ge(ratio_done, q)
                act.activation(two(buf_a, r), block_of(later, blk), ACT.Exp, scale=a_n[:, 0:1]).then_inc(cum_done, 1)
                act.wait_ge(cum_done, q + 1)
                act.activation(two(buf_b, r), two(buf_a, r), ACT.Ln, bias=eps[:, 0:1]).then_inc(lnc_done, 1)
                act.wait_ge(lnc_done, q + 1)
                act.activation(two(buf_b, r), two(buf_b, r), ACT.Exp, scale=-1.0).then_inc(rec_done, 1)

            def skip(n):
                act.sem_inc(cum_done, n)
                act.sem_inc(lnc_done, n)
                act.sem_inc(rec_done, n)

            with act.Fori(0, NS) as n:
                act.wait_ge(rep_staged, n * 3 + 3)
                blocks(act, act.value_load, n, body, skip)
            act.wait_ge(y_added, NS * BLOCKS)
            tail = later[:, :].rearrange("p (a t) -> p a t", a=2)[:, :, L - TAIL:L]
            for n in range(NS):
                e = act.activation(buf_a[:, n * P:n * P + P].rearrange("p (a t) -> p a t", a=2), tail,
                                   ACT.Exp, scale=a_neg[:, n:n + 1])
            e.then_inc(cum_done, 1)
            act.wait_ge(cum_done, NS * BLOCKS + 1)
            act.activation(buf_b[:, :], buf_a[:, :], ACT.Ln, bias=eps[:, 0:1]).then_inc(lnc_done, 1)
            act.wait_ge(lnc_done, NS * BLOCKS + 1)
            act.activation(buf_b[:, :], buf_b[:, :], ACT.Exp, scale=-1.0).then_inc(rec_done, 1)

        @block.vector
        def _(dve):
            def body(q, blk, r):
                dve.wait_ge(bc_done, q + 1)
                dve.wait_ge(duc_done, q + 1)
                a, c = two(buf_a, r), two(buf_c, r)
                dve.tensor_tensor(a, a, psum[:, 4 * r:4 * r + 2, 0:BLK], ALU.mult).then_inc(term_done, 1)
                dve.wait_ge(term_done, q + 1)
                dve.wait_ge(y_added, q)
                for half in range(HALVES):
                    m = dve.tensor_tensor_scan(c[:, half, :], ones[:, 0:1].to_broadcast([P, BLK]), a[:, half, :],
                                               state[:, half:half + 1], ALU.mult, ALU.add)
                m.then_inc(sum_done, 1)
                dve.wait_ge(sum_done, q + 1)
                dve.tensor_copy(state[:, :], c[:, :, BLK - 1]).then_inc(state_set, 1)
                dve.wait_ge(rec_done, q + 1)
                dve.wait_ge(state_set, q + 1)
                dve.tensor_tensor(c, c, two(buf_b, r), ALU.mult).then_inc(ratio_done, 1)
                dve.wait_ge(ratio_done, q + 1)
                dve.tensor_tensor(c, c, psum[:, 4 * r + 2:4 * r + 4, 0:BLK], ALU.mult).then_inc(out_done, 1)

            def skip(n):
                for s in (term_done, sum_done, state_set, ratio_done, out_done):
                    dve.sem_inc(s, n)

            with dve.Fori(0, NS) as n:
                dve.memset(state[:, :], 0.0).then_inc(state_kept, 1)
                dve.wait_ge(state_kept, n * 2 + 1)
                blocks(dve, dve.value_load, n, body, skip)
                dve.tensor_copy(carry[:, :, bass.ds(n, 1)], state[:, :].unsqueeze(2)).then_inc(state_kept, 1)
                dve.wait_ge(state_kept, n * 2 + 2)
            done = NS * BLOCKS
            all_n = buf_a[:, :].rearrange("p (n a t) -> p n a t", n=NS, a=2)
            tail = du[:, :].rearrange("p (a t) -> p a t", a=2)[:, :, L - TAIL:L]
            dve.wait_ge(lnc_done, done + 1)
            dve.tensor_tensor(all_n, all_n, tail.unsqueeze(1).broadcast_to([P, NS, 2, TAIL]), ALU.mult
                              ).then_inc(term_done, 1)
            dve.wait_ge(term_done, done + 1)
            dve.wait_ge(bc_done, done + 1)
            dve.tensor_tensor(buf_a[:, :], buf_a[:, :], psum[:, 0:4, :].rearrange("p b n -> p (b n)"), ALU.mult
                              ).then_inc(term_done, 1)
            dve.wait_ge(term_done, done + 2)
            dve.tensor_tensor(all_n[:, :, :, 0], all_n[:, :, :, 0], carry[:, :, :].rearrange("p a n -> p n a"),
                              ALU.add).then_inc(term_done, 1)
            dve.wait_ge(term_done, done + 3)
            for m in range(4):
                s = dve.tensor_tensor_scan(buf_c[:, m * 512:m * 512 + 512], kc[:, K_SEG:K_SEG + 512],
                                           buf_a[:, m * 512:m * 512 + 512], 0.0, ALU.mult, ALU.add)
            s.then_inc(sum_done, 1)
            dve.wait_ge(sum_done, done + 1)
            dve.wait_ge(rec_done, done + 1)
            dve.tensor_tensor(buf_c[:, :], buf_c[:, :], buf_b[:, :], ALU.mult).then_inc(ratio_done, 1)
            dve.wait_ge(ratio_done, done + 1)
            dve.wait_ge(bc_done, done + 2)
            dve.tensor_tensor(buf_c[:, :], buf_c[:, :], psum[:, 4:8, :].rearrange("p b n -> p (b n)"), ALU.mult
                              ).then_inc(out_done, 1)
            dve.wait_ge(out_done, done + 1)
            dve.tensor_reduce(buf_b[:, 0:P], buf_c[:, :].rearrange("p (n x) -> p x n", n=NS), AX.X, ALU.add
                              ).then_inc(carried, 1)
            dve.wait_ge(carried, 1)
            y_tail = y[:, :].rearrange("p (a t) -> p a t", a=2)[:, :, L - TAIL:L]
            dve.tensor_tensor(y_tail, y_tail, buf_b[:, 0:P].rearrange("p (a t) -> p a t", a=2), ALU.add
                              ).then_inc(carried, 1)


def backwards(arr, at, n, p):
    ap = arr[:, at + n - 1:at + n]
    return bass.AP(tensor=ap.tensor, offset=ap.offset, ap=[list(ap.ap[0]), [-1, n]])


def store_quad(eng, out, src, i, done):
    at = i // 2 * 512 + i % 2 * 32 + i // 16 * L
    flat = out.rearrange("b t d -> (b t) d")
    for k in range(2):
        for b2 in range(2):
            a = flat[bass.ds(at + (k * 16 + b2 * L), 1), :]
            dst = bass.AP(tensor=a.tensor, offset=a.offset, ap=[[SIDE * C, 8], [C, 16], [1, C]],
                          dep_tracking_offset=a.dep_tracking_offset)
            eng.dma_start(dst, src[:, 2 * k + b2, :]).then_inc(done, 16)


def experts(nc, ctx, kc, psum, y, h_all, ident, moe, out):
    router_w, router_b, w1, b1, w2, b2 = moe

    def sb(name, shape, dt=F32):
        return ctx.enter_context(nc.sbuf_tensor(name, shape, dt))

    def sem(name):
        return ctx.enter_context(nc.semaphore(name))

    w1x = sb("w1x", [P, NE, HID])
    w2x = sb("w2x", [P, 4, C])
    b2x = sb("b2x", [P, C])
    rw = sb("rw", [NE, C])
    rwx = sb("rwx", [C + 1, NE])
    y_st = sb("y_st", [P, 2, P])
    nsum = sb("m_nsum", [P, 4])
    xc = sb("m_xc", [P, 4, C])
    sq = sb("m_sq", [P, 4, C])
    ssum = sb("m_ssum", [P, 4])
    var = sb("m_var", [P, 4])
    mhalf = sb("m_mhalf", [P, 4])
    rstd = sb("m_rstd", [P, 4])
    comb = sb("comb", [P, 4, P])
    x1 = sb("x1", [C + 1, 4 * P])
    comb_t = sb("comb_t", [P, 4 * P])
    best = sb("best", [P, 4])
    h_seen = sb("h_seen", [P, 1])
    is_best = sb("is_best", [P, 4, NE])
    rank = sb("rank", [P, 4, NE])
    best_rank = sb("best_rank", [P, 4])
    hid = sb("hid", [P, 4, 4 * P])
    out_st = sb("out_st", [P, 4, C])

    w_in, wset, rw_turned = sem("m_w_in"), sem("m_wset"), sem("rw_turned")
    prep, power_set = sem("m_prep"), sem("m_power_set")
    y_staged, y_turned, h_done = sem("y_staged"), sem("y_turned"), sem("m_h_done")
    nsum_done, xc_done, sq_done, ssum_done = sem("m_nsum_done"), sem("m_xc_done"), sem("m_sq_done"), sem("m_ssum_done")
    var_done, rstd_done, xh_done = sem("m_var_done"), sem("m_rstd_done"), sem("m_xh_done")
    x_turned, x_copied, logits_done = sem("m_x_turned"), sem("m_x_copied"), sem("logits_done")
    best_done, eq_done, rank_done, chosen = sem("best_done"), sem("eq_done"), sem("rank_done"), sem("chosen")
    mark_done, comb_turned, comb_copied = sem("mark_done"), sem("comb_turned"), sem("comb_copied")
    hid_done, relu_act, relu_dve = sem("hid_done"), sem("relu_act"), sem("relu_dve")
    bias_done, o_done, out_made, stored = sem("bias_done"), sem("m_o_done"), sem("out_made"), sem("stored")

    LAST = QUADS + 2
    HID_BANK = (4, 5, 7, 4)

    def steps(eng, body):
        for i in range(4):
            body(i)
        with eng.Fori(4, QUADS) as i:
            body(i)
        for i in range(QUADS, LAST + 1):
            body(i)

    def live(i, lag):
        return not isinstance(i, int) or 0 <= i - lag < QUADS

    def first(i, lag=0):
        return isinstance(i, int) and i - lag <= 0

    with nc.Block() as block:
        @block.sync
        def _(sp):
            sp.dma_start(w1x[0:C, :, :], w1.rearrange("e d h -> d e h")).then_inc(w_in, 16)
            sp.dma_start(w1x[96:P, :, :], b1.partition_broadcast(NE)).then_inc(w_in, 16)
            sp.dma_start(w2x[:, :, :], w2.rearrange("(g e) h d -> (e h) g d", g=4)).then_inc(w_in, 16)
            sp.dma_start(rw[:, :], router_w).then_inc(w_in, 16)
            sp.dma_start(rwx[C:C + 1, :], router_b.rearrange("(o e) -> o e", o=1)).then_inc(w_in, 16)
            sp.wait_ge(wset, 1)
            sp.dma_start(b2x[96:P, :], b2).then_inc(w_in, 16)
            for i in range(1):
                sp.wait_ge(out_made, i + 1)
                store_quad(sp, out, out_st[:, :, :], i, stored)
            with sp.Fori(1, QUADS) as i:
                sp.wait_ge(out_made, i + 1)
                store_quad(sp, out, out_st[:, :, :], i, stored)
            sp.wait_ge(stored, QUADS * 64)

        @block.gpsimd
        def _(pool):
            pool.memset(b2x[:, :], 0.0).then_inc(wset, 1)
            pool.memset(mhalf[:, :], -0.5).then_inc(power_set, 1)
            pool.wait_ge(power_set, 1)
            pool.memset(x1[C:C + 1, :], 1.0).then_inc(power_set, 1)
            pool.wait_ge(power_set, 2)

            def body(i):
                if not live(i, 0):
                    return
                pool.wait_ge(xc_done, i + 1)
                pool.tensor_tensor(sq[:, :, :], xc[:, :, :], xc[:, :, :], ALU.mult).then_inc(sq_done, 1)
                pool.wait_ge(var_done, i + 1)
                pool.tensor_tensor(rstd[:, :], var[:, :], mhalf[:, :], ALU.pow).then_inc(rstd_done, 1)
                pool.wait_ge(rstd_done, i + 1)
                if not first(i):
                    pool.wait_ge(comb_turned, i)
                pool.tensor_tensor(comb[:, :, 0:C], xc[:, :, :], rstd[:, :].unsqueeze(2).broadcast_to([P, 4, C]),
                                   ALU.mult).then_inc(xh_done, 1)

            steps(pool, body)

        @block.tensor
        def _(pe):
            pe.wait_ge(w_in, 16 * 6)
            pe.transpose(psum[0:C, 7, 0:NE], rw[:, :], kc[0:NE, 0:NE]).then_inc(rw_turned, 1)
            pe.wait_ge(prep, 5)
            pe.wait_ge(power_set, 2)

            def hidden(i, g):
                if g == 3:
                    pe.wait_ge(relu_act, i * 3 + 1)
                elif not first(i):
                    pe.wait_ge(relu_act, i * 3)
                    pe.wait_ge(relu_dve, i)
                pe.matmul(psum[:, HID_BANK[g], :], w1x[:, g * 8:g * 8 + 8, :], comb_t[:, :],
                          start=True, stop=True).then_inc(hid_done, 1)

            def body(i):
                if live(i, 1):
                    pe.wait_ge(xh_done, i)
                    if not first(i, 1):
                        pe.wait_ge(x_copied, i - 1)
                if live(i, 0):
                    pe.wait_ge(y_staged, i + 1)
                    if not first(i):
                        pe.wait_ge(h_done, i)
                    for n in range(2):
                        m = pe.transpose(psum[:, 0, n * P:n * P + P], y_st[:, n, :], ident)
                    m.then_inc(y_turned, 1)
                if live(i, 1):
                    for s in range(4):
                        m = pe.transpose(psum[0:C, 1, s * P:s * P + P], comb[:, s, 0:C], ident)
                    m.then_inc(x_turned, 1)
                if live(i, 2):
                    pe.wait_ge(comb_copied, i - 1)
                    hidden(i - 2, 0)
                if live(i, 1):
                    pe.wait_ge(x_copied, i)
                    if not first(i, 1):
                        pe.wait_ge(eq_done, i - 1)
                    for s in range(4):
                        m = pe.matmul(psum[:, 2, s * NE:s * NE + NE], x1[:, s * P:s * P + P], rwx[:, :],
                                      start=True, stop=True, skip_group_check=True)
                    m.then_inc(logits_done, 1)
                if live(i, 2):
                    hidden(i - 2, 1)
                    hidden(i - 2, 2)
                    hidden(i - 2, 3)
                    if not first(i, 2):
                        pe.wait_ge(out_made, i - 2)
                    for s in range(4):
                        m = pe.matmul(psum[:, 6, s * C:s * C + C], comb_t[:, s * P:s * P + P], b2x[:, :],
                                      start=(s == 0), stop=False, skip_group_check=True)
                    m.then_inc(bias_done, 1)
                if live(i, 1):
                    pe.wait_ge(chosen, i)
                    if not first(i, 1):
                        pe.wait_ge(comb_copied, i - 1)
                    for s in range(4):
                        m = pe.transpose(psum[:, 3, s * P:s * P + P], comb[:, s, :], ident)
                    m.then_inc(comb_turned, 1)
                if live(i, 2):
                    pe.wait_ge(relu_act, i * 3 - 3)
                    pe.wait_ge(relu_dve, i - 1)
                    for s in range(4):
                        for g in range(4):
                            m = pe.matmul(psum[:, 6, s * C:s * C + C], hid[:, g, s * P:s * P + P], w2x[:, g, :],
                                          start=False, stop=(g == 3), skip_group_check=True)
                    m.then_inc(o_done, 1)

            steps(pe, body)

        @block.scalar
        def _(act):
            def stage_y(i):
                if not first(i):
                    act.wait_ge(y_turned, i)
                a = act.activation(y_st[:, :, :].rearrange("p k (r x) -> p k r x", r=8),
                                   raster(y, i // 2 * 512 + i % 2 * 32), ACT.Copy)
                a.then_inc(y_staged, 1)

            def relu(i, g):
                act.wait_ge(hid_done, i * 4 + (g + 1))
                if not first(i):
                    act.wait_ge(o_done, i)
                act.activation(hid[:, g, :], psum[:, HID_BANK[g], :], ACT.Relu).then_inc(relu_act, 1)

            def body(i):
                if live(i, 0):
                    stage_y(i)
                if live(i, 1):
                    act.wait_ge(x_turned, i)
                    if not first(i, 1):
                        act.wait_ge(logits_done, i - 1)
                    act.activation(x1[0:C, :], psum[0:C, 1, :], ACT.Copy).then_inc(x_copied, 1)
                if live(i, 2):
                    relu(i - 2, 0)
                    relu(i - 2, 1)
                    relu(i - 2, 3)
                if live(i, 1):
                    act.wait_ge(comb_turned, i)
                    if not first(i, 1):
                        act.wait_ge(bias_done, i - 1)
                    act.activation(comb_t[:, :], psum[:, 3, :], ACT.Copy).then_inc(comb_copied, 1)

            steps(act, body)

        @block.vector
        def _(dve):
            eye = kc[:, K_EYE:K_EYE + NE].unsqueeze(2).to_broadcast([P, NE, HID])
            dve.wait_ge(w_in, 16 * 6)
            dve.tensor_scalar(w1x[64:96, :, :], eye[64:96], BIG, None, ALU.mult).then_inc(prep, 1)
            dve.tensor_tensor(w1x[96:P, :, :], w1x[96:P, :, :], eye[96:P], ALU.mult).then_inc(prep, 1)
            dve.wait_ge(rw_turned, 1)
            dve.tensor_copy(rwx[0:C, :], psum[0:C, 7, 0:NE]).then_inc(prep, 3)

            def body(i):
                if live(i, 3):
                    dve.wait_ge(o_done, i - 2)
                    if not first(i, 3):
                        dve.wait_ge(stored, i * 64 - 192)
                    dve.scalar_tensor_tensor(out_st[:, :, :].rearrange("p s d -> p (s d)"), psum[:, 6, 0:256], 0.0,
                                             h_all[:, bass.ds(i * 4 - 12, 4), :].rearrange("p s d -> p (s d)"),
                                             ALU.max, ALU.add).then_inc(out_made, 1)
                if live(i, 0):
                    h = h_all[:, bass.ds(i * 4, 4), :]
                    dve.wait_ge(y_turned, i + 1)
                    dve.tensor_tensor(h, h, psum[:, 0, 0:256].rearrange("p (s d) -> p s d", s=4), ALU.add
                                      ).then_inc(h_done, 1)
                    dve.wait_ge(h_done, i + 1)
                    dve.memset(h_seen[:, :], 0.0)
                    dve.tensor_reduce(nsum[:, :], h, AX.X, ALU.add, negate=True).then_inc(nsum_done, 1)
                    dve.wait_ge(nsum_done, i + 1)
                    if not first(i):
                        dve.wait_ge(xh_done, i)
                    dve.scalar_tensor_tensor(xc[:, :, :], nsum[:, :].unsqueeze(2).broadcast_to([P, 4, C]),
                                             1.0 / C, h, ALU.mult, ALU.add).then_inc(xc_done, 1)
                if live(i, 1):
                    lg = psum[:, 2, 0:4 * NE].rearrange("p (s e) -> p s e", s=4)
                    dve.wait_ge(logits_done, i)
                    dve.tensor_reduce(best[:, :], lg, AX.X, ALU.max).then_inc(best_done, 1)
                    dve.wait_ge(best_done, i * 2 - 1)
                    dve.tensor_tensor(is_best[:, :, :], lg, best[:, :].unsqueeze(2).broadcast_to([P, 4, NE]),
                                      ALU.is_equal).then_inc(eq_done, 1)
                    dve.wait_ge(eq_done, i)
                    dve.tensor_tensor(rank[:, :, :], is_best[:, :, :],
                                      kc[:, K_REV:K_REV + NE].unsqueeze(1).broadcast_to([P, 4, NE]), ALU.mult
                                      ).then_inc(rank_done, 1)
                    dve.wait_ge(rank_done, i)
                    dve.tensor_reduce(best_rank[:, :], rank[:, :, :], AX.X, ALU.max).then_inc(best_done, 1)
                    dve.wait_ge(best_done, i * 2)
                    if not first(i, 1):
                        dve.wait_ge(comb_turned, i - 1)
                    dve.tensor_tensor(comb[:, :, 96:P], rank[:, :, :],
                                      best_rank[:, :].unsqueeze(2).broadcast_to([P, 4, NE]), ALU.is_equal
                                      ).then_inc(mark_done, 1)
                    dve.wait_ge(mark_done, i)
                    dve.tensor_scalar(comb[:, :, C:96], comb[:, :, 96:P], -1.0, None, ALU.add).then_inc(chosen, 1)
                if live(i, 2):
                    dve.wait_ge(hid_done, i * 4 - 5)
                    if not first(i, 2):
                        dve.wait_ge(o_done, i - 2)
                    dve.tensor_scalar(hid[:, 2, :], psum[:, HID_BANK[2], :], 0.0, None, ALU.max).then_inc(relu_dve, 1)
                if live(i, 0):
                    dve.wait_ge(sq_done, i + 1)
                    dve.tensor_reduce(ssum[:, :], sq[:, :, :], AX.X, ALU.add).then_inc(ssum_done, 1)
                    dve.wait_ge(ssum_done, i + 1)
                    dve.tensor_scalar(var[:, :], ssum[:, :], 1.0 / C, LN_EPS, ALU.mult, ALU.add
                                      ).then_inc(var_done, 1)

            steps(dve, body)




_INS = ['x', 'L0_tok_qkv_w', 'L0_tok_qkv_b', 'L0_tok_proj_w', 'L0_tok_proj_b', 'L0_attn_W_dbc',
        'L0_attn_W_dt', 'L0_attn_b_dt', 'L0_attn_A_log', 'L0_attn_D', 'L0_ffn_router_w',
        'L0_ffn_router_b', 'L0_ffn_W1', 'L0_ffn_b1', 'L0_ffn_W2', 'L0_ffn_b2']


def constants():
    import numpy as np
    k = np.zeros((P, K_END), np.float32)
    k[:, K_IDENT:K_IDENT + P] = np.eye(P)
    p = np.arange(P)
    d = p % 4
    k[p ^ 1, K_SWAP + p] = 1.0
    freq = (1.0 / 10000.0 ** (np.arange(0, 4, 2, dtype=np.float32) / 4)).astype(np.float32)
    ang = np.arange(8, dtype=np.float32)[:, None] * freq
    cos, sin = np.cos(ang).astype(np.float32), np.sin(ang).astype(np.float32)
    cos4 = np.repeat(cos, 2, axis=1)
    sin4 = np.stack([-sin, sin], axis=-1).reshape(8, 4)
    k[:, K_COSC:K_COSC + 8] = cos4[:, d].T
    k[:, K_SINC:K_SINC + 8] = sin4[:, d].T
    k[:, K_COSR:K_COSR + 32] = cos4.reshape(-1)
    k[:, K_SINR:K_SINR + 32] = sin4.reshape(-1)
    k[p, K_HEAD + p % 32 // 4] = 1.0
    k[:, K_REV:K_REV + NE] = NE - np.arange(NE)
    seg = np.ones((8, TAIL), np.float32)
    seg[:, 0] = 0.0
    k[:, K_SEG:K_SEG + 8 * TAIL] = seg.reshape(-1)
    k[p, K_EYE + p % NE] = 1.0
    for w in range(2):
        k[:, K_WIN + w] = p // 32 % 2 == w
    return k


def kernel(**inputs):
    import numpy as np
    import concourse.bacc as bacc
    from concourse.bass_utils import run_bass_kernel_spmd

    nc = bacc.Bacc("TRN2", target_bir_lowering=False, num_devices=1)
    arrays, args = {}, []
    for name in _INS:
        a = np.ascontiguousarray(inputs[name])
        arrays[f"in_{name}"] = a
        args.append(nc.dram_tensor(f"in_{name}", a.shape, mybir.dt.from_np(a.dtype), kind="ExternalInput").ap())
    arrays["constants"] = constants()
    args.append(nc.dram_tensor("constants", (P, K_END), F32, kind="ExternalInput").ap())
    args.append(nc.dram_tensor("out_0", (BATCH, L, C), F32, kind="ExternalOutput").ap())
    vit_layer(nc, *args)
    r = run_bass_kernel_spmd(nc, [arrays], core_ids=[0])
    return r.results[0]["out_0"]
```

```python
from contextlib import ExitStack

import concourse.bass as bass
from concourse import mybir

F32 = mybir.dt.float32
I32 = mybir.dt.int32
ALU = mybir.AluOpType
ACT = mybir.ActivationFunctionType
AX = mybir.AxisListType

P = 128
C = 64
NH, HD = 8, 8
SIDE = 64
L = SIDE * SIDE
BATCH = 4
HALVES = 2
SLOTS = BATCH * L // P
QUADS = SLOTS // 4
CHUNKS = 8
WIN = 64
NS = 16
RANK = 16
NE, HID = 32, 16
BIG = 1e30
SCALE = float(HD) ** -0.5
LN_EPS = 1e-5
SCAN_EPS = 1e-12
TAIL = 64
BLK = 448
BLOCKS = (L - TAIL) // BLK
SLOW = 2
EXP_ZERO = -104.0

K_IDENT = 0
K_SWAP = K_IDENT + P
K_COSC = K_SWAP + P
K_SINC = K_COSC + 8
K_HEAD = K_SINC + 8
K_COSR = K_HEAD + NH
K_SINR = K_COSR + 32
K_REV = K_SINR + 32
K_SEG = K_REV + NE
K_EYE = K_SEG + 8 * TAIL
K_WIN = K_EYE + NE
K_END = K_WIN + 2


def vit_layer(nc, x, qkv_w, qkv_b, proj_w, proj_b, w_dbc, w_dt, b_dt, a_log, d_skip,
              router_w, router_b, w1, b1, w2, b2, consts, out):
    ctx = ExitStack()
    with ctx:
        def sb(name, shape, dt=F32):
            return ctx.enter_context(nc.sbuf_tensor(name, shape, dt))

        def sem(name):
            return ctx.enter_context(nc.semaphore(name))

        psum = ctx.enter_context(nc.psum_tensor("psum", [P, 8, 512], F32))
        banks = [psum[:, i, :] for i in range(8)]

        kc = sb("kc", [P, K_END])
        h_all = sb("h_all", [P, SLOTS, C])
        big_a = sb("big_a", [P, HALVES * L])
        big_b = sb("big_b", [P, HALVES * L])
        big_c = sb("big_c", [P, HALVES * L])
        u_all = sb("u_all", [P, HALVES * L])
        w_v = sb("w_v", [P, P])
        w_proj = sb("w_proj", [P, P])
        pb_row = sb("pb_row", [P, C])
        bv_col = sb("bv_col", [P, 1])
        wd = sb("wd", [P, RANK + 2 * NS])
        w_delta = sb("w_delta", [P, P])
        b_col = sb("b_col", [P, 1])
        d_col = sb("d_col", [P, 1])
        a_neg = sb("a_neg", [P, NS])

        ident = kc[:, K_IDENT:K_IDENT + P]
        xT, qT, kT = big_a, big_b, big_c

        def dup(eng, dst, src, s):
            for half in range(2):
                eng.dma_start(dst[64 * half:64 * half + 64], src).then_inc(s, 16)

        with ExitStack() as st1:
            def sb1(name, shape, dt=F32):
                return st1.enter_context(nc.sbuf_tensor(name, shape, dt))

            w_qkv_t = sb1("w_qkv_t", [P, 3 * C])
            wdt = sb1("wdt", [RANK, C])
            wd_t = sb1("wd_t", [RANK, P])
            wraw = sb1("wraw", [P, 2, C])
            wraw2 = sb1("wraw2", [C, 2, C])
            praw = sb1("praw", [C, 2, C])
            w_swap = sb1("w_swap", [P, 2 * C])
            rot = sb1("rot", [P, 2, 2, 8, 2, 32])
            rtmp = sb1("rtmp", [P, 2, 8, 32])
            bqk = sb1("bqk", [P, 2])
            bqk_swap = sb1("bqk_swap", [P, 2])
            rbias = sb1("rbias", [P, 2, 8])
            rb_t = sb1("rb_t", [P, 8])

            scan_in, wd_zeroed, a_done = sem("scan_in"), sem("wd_zeroed"), sem("a_done")
            wdt_turned, wdt_copied, wd_done, wd_copied = (
                sem("wdt_turned"), sem("wdt_copied"), sem("wd_done"), sem("wd_copied"))
            kc_in, w_in, bqk_in, row_in = sem("kc_in"), sem("w_in"), sem("bqk_in"), sem("row_in")
            x_in = [sem(f"x_in{s}") for s in range(CHUNKS)]
            zeroed, wt_done, wt_copied = sem("zeroed"), sem("wt_done"), sem("wt_copied")
            prep, bias_ready, rot_ready = sem("prep"), sem("bias_ready"), sem("rot_ready")
            x_turned, x_left, x_right = sem("x_turned"), sem("x_left"), sem("x_right")
            rot_made = sem("rot_made")
            qk_done, q_left, q_right = sem("qk_done"), sem("q_left"), sem("q_right")

            xin = h_all[:, :, :]

            def copy_x(eng, op, n, w, *kind):
                rho, j, c4 = n // 8, n // 2 % 4, n % 2
                eng.wait_ge(x_turned, 2 * n + w + 1)
                at = j * WIN + rho * 8 + c4 * 4
                a = xT[64 * w:64 * w + 64, at:at + 1]
                dst = bass.AP(tensor=a.tensor, offset=a.offset,
                              ap=[list(a.ap[0]), [1, 4], [4 * WIN, 32], [16, 4]])
                bank = banks[4 * w + n % 4]
                return op(dst, bank[0:64, :].rearrange("p (c a b) -> p c a b", c=4, a=32), *kind)

            with nc.Block() as block:
                @block.sync
                def _(sp):
                    sp.dma_start(kc[:, :], consts).then_inc(kc_in, 16)
                    rows = x.rearrange("b (a z) col d -> (b a) (z col) d", z=2)
                    for ch in range(CHUNKS):
                        sp.dma_start(xin[:, ch * 16:ch * 16 + 16, :], rows[:, ch * 16:ch * 16 + 16, :]
                                     ).then_inc(x_in[ch], 16)
                    dup(sp, wd, w_dbc, scan_in)
                    dup(sp, b_col, b_dt.rearrange("(d o) -> d o", o=1), scan_in)
                    dup(sp, d_col, d_skip.rearrange("(d o) -> d o", o=1), scan_in)
                    dup(sp, a_neg, a_log, scan_in)
                    sp.dma_start(wdt[:, :], w_dt).then_inc(scan_in, 16)

                @block.scalar
                def _(act):
                    for d in range(2):
                        act.dma_start(wraw[:, d, :], qkv_w[0:2 * C, :]).then_inc(w_in, 16)
                        act.dma_start(wraw2[:, d, :], qkv_w[2 * C:3 * C, :]).then_inc(w_in, 16)
                        act.dma_start(praw[:, d, :], proj_w).then_inc(w_in, 16)
                    act.dma_start(pb_row[:, :], proj_b.partition_broadcast(P)).then_inc(row_in, 16)
                    dup(act, bv_col, qkv_b[2 * C:3 * C].rearrange("(d o) -> d o", o=1), row_in)
                    act.preload_act_table_set("natural_log_exp_and_others")
                    for n in range(16):
                        copy_x(act, act.activation, n, 0, ACT.Copy).then_inc(x_left, 1)
                    for half in range(2):
                        if half == 0:
                            act.wait_ge(bias_ready, 1)
                        for n in range(16):
                            qk, v = n // 8, n % 8
                            dst = (qT, kT)[qk][0:64, half * L:half * L + L].rearrange(
                                "p (s r c) -> p s r c", r=8, c=8)[:, :, v, :]
                            act.wait_ge(qk_done, half * 16 + n + 1)
                            act.activation(dst, banks[4 + n % 4][0:64, :].rearrange("p (s c) -> p s c", c=8),
                                           ACT.Identity, bias=rbias[0:64, qk, v:v + 1],
                                           scale=SCALE if qk == 0 else 1.0).then_inc(q_left, 1)

                    act.wait_ge(scan_in, 16 * 9)
                    act.activation(a_neg[:, :], a_neg[:, :], ACT.Exp).then_inc(a_done, 1)
                    act.wait_ge(row_in, 48)

                @block.gpsimd
                def _(pool):
                    for qk in range(2):
                        for eta in range(2):
                            for w in range(2):
                                src = qkv_b[qk * C:qk * C + C].rearrange(
                                    "(h e d o) -> h e d o", e=2, d=4, o=1)[:, eta]
                                p0 = eta * 64 + w * 32
                                pool.dma_start(bqk[p0:p0 + 32, qk:qk + 1], src).then_inc(bqk_in, 16)
                    pool.memset(rot[:, :, :, :, :, :], 0.0).then_inc(zeroed, 1)
                    pool.memset(w_v[:, :], 0.0).then_inc(zeroed, 1)
                    pool.memset(w_proj[:, :], 0.0).then_inc(zeroed, 1)
                    pool.memset(w_delta[:, :], 0.0).then_inc(wd_zeroed, 1)
                    pool.wait_ge(wt_copied, 3)
                    pool.wait_ge(prep, 2)
                    done = 0
                    for qk in range(2):
                        for eta in range(2):
                            def part(src):
                                v = src[:, qk * C:qk * C + C].rearrange("p (h e d) -> p h e d", e=2, d=4)
                                return v[:, :, eta, :].unsqueeze(1).broadcast_to([P, 8, 8, 4])

                            def trig(at):
                                v = kc[:, at:at + 32].rearrange("p (v d) -> p v d", d=4)
                                return v.unsqueeze(2).broadcast_to([P, 8, 8, 4])

                            dst = [rtmp[:, i].rearrange("p v (h d) -> p v h d", d=4) for i in range(2)]
                            pool.tensor_tensor(dst[0], part(w_qkv_t), trig(K_COSR), ALU.mult).then_inc(rot_made, 1)
                            pool.tensor_tensor(dst[1], part(w_swap), trig(K_SINR), ALU.mult).then_inc(rot_made, 1)
                            done += 2
                            pool.wait_ge(rot_made, done)
                            for w in range(2):
                                q = slice(64 * w, 64 * w + 64)
                                i = pool.tensor_tensor(rot[q, qk, eta, :, w, :], rtmp[q, 0], rtmp[q, 1], ALU.add)
                                i.then_inc(rot_made, 1)
                            done += 2
                            pool.wait_ge(rot_made, done)
                            pool.sem_inc(rot_ready, 1)

                @block.tensor
                def _(pe):
                    pe.wait_ge(kc_in, 16)
                    pe.wait_ge(w_in, 16 * 6)
                    pe.transpose(banks[2][:, 0:P], wraw[:, :, :], ident)
                    pe.transpose(banks[2][:, P:P + C], wraw2[:, :, :], kc[0:C, 0:C])
                    pe.transpose(banks[2][:, P + C:2 * P], praw[:, :, :], kc[0:C, 0:C]).then_inc(wt_done, 1)
                    pe.wait_ge(bqk_in, 16 * 8)
                    pe.matmul(banks[3][:, 0:2], kc[:, K_SWAP:K_SWAP + P], bqk[:, :],
                              start=True, stop=True).then_inc(wt_done, 1)
                    pe.wait_ge(prep, 3)
                    for n in range(16):
                        rho, j, c4 = n // 8, n // 2 % 4, n % 2
                        pe.wait_ge(x_in[rho * 4 + j], 16)
                        for w in range(2):
                            if n >= 4:
                                pe.wait_ge((x_left, x_right)[w], n - 3)
                            for c in range(4):
                                t0 = rho * SIDE + j * 16 + w * 8 + c4 * 4 + c
                                t = pe.transpose(banks[4 * w + n % 4][0:64, c * P:c * P + P], xin[:, t0, :], ident)
                            t.then_inc(x_turned, 1)
                    pe.wait_ge(x_left, 16)
                    pe.wait_ge(x_right, 16)
                    pe.wait_ge(scan_in, 16 * 9)
                    pe.transpose(banks[0][0:RANK, 0:P], wd[:, 0:RANK], ident).then_inc(wdt_turned, 1)
                    for half in range(2):
                        if half == 1:
                            pe.wait_ge(wdt_copied, 1)
                            pe.matmul(banks[1][:, 0:C], wd_t[:, :], wdt[:, :], start=True, stop=True
                                      ).then_inc(wd_done, 1)
                        pe.wait_ge(rot_ready, 4)
                        xh = xT[:, half * L:half * L + L].rearrange("p (s r c) -> p s r c", r=8, c=8)
                        for n in range(16):
                            qk, v = n // 8, n % 8
                            m = half * 16 + n
                            if m >= 4:
                                pe.wait_ge(q_left, m - 3)
                                pe.wait_ge(q_right, m - 3)
                            bank = banks[4 + n % 4]
                            pe.matmul(bank[0:64, :], rot[:, qk, 0, v], xh[:, :, v, :],
                                      start=True, stop=True)
                            pe.matmul(bank[64:128, :], rot[:, qk, 1, v], xh[:, :, :, v],
                                      start=True, stop=True).then_inc(qk_done, 1)

                @block.vector
                def _(dve):
                    dve.wait_ge(zeroed, 3)
                    dve.wait_ge(wt_done, 1)
                    dve.tensor_copy(w_qkv_t[:, :], banks[2][:, 0:3 * C]).then_inc(wt_copied, 1)
                    for w in range(2):
                        q = slice(64 * w, 64 * w + 64)
                        dve.tensor_copy(w_proj[q, q], banks[2][q, 3 * C:4 * C]).then_inc(wt_copied, 1)
                    dve.wait_ge(wt_copied, 3)
                    for w in range(2):
                        q = slice(64 * w, 64 * w + 64)
                        dve.tensor_copy(w_v[q, q], w_qkv_t[q, 2 * C:3 * C])
                    pairs = w_qkv_t[:, 0:2 * C].rearrange("p (n e) -> p n e", e=2)
                    swaps = w_swap[:, :].rearrange("p (n e) -> p n e", e=2)
                    dve.tensor_copy(swaps[:, :, 0], pairs[:, :, 1]).then_inc(prep, 1)
                    dve.tensor_copy(swaps[:, :, 1], pairs[:, :, 0]).then_inc(prep, 1)
                    dve.wait_ge(wt_done, 2)
                    dve.tensor_copy(bqk_swap[:, :], banks[3][:, 0:2]).then_inc(prep, 1)
                    dve.wait_ge(prep, 3)
                    done = 3
                    for qk in range(2):
                        dve.tensor_scalar(rb_t[:, :], kc[:, K_COSC:K_COSC + 8], bqk[:, qk:qk + 1],
                                          SCALE if qk == 0 else 1.0, ALU.mult, ALU.mult).then_inc(prep, 1)
                        dve.tensor_scalar(rbias[:, qk, :], kc[:, K_SINC:K_SINC + 8], bqk_swap[:, qk:qk + 1],
                                          SCALE if qk == 0 else 1.0, ALU.mult, ALU.mult).then_inc(prep, 1)
                        done += 2
                        dve.wait_ge(prep, done)
                        dve.tensor_tensor(rbias[:, qk, :], rbias[:, qk, :], rb_t[:, :], ALU.add).then_inc(prep, 1)
                        done += 1
                        dve.wait_ge(prep, done)
                    dve.sem_inc(bias_ready, 1)
                    for n in range(16):
                        copy_x(dve, dve.tensor_copy, n, 1).then_inc(x_right, 1)
                    for half in range(2):
                        for n in range(16):
                            qk, v = n // 8, n % 8
                            dst = (qT, kT)[qk][64:128, half * L:half * L + L].rearrange(
                                "p (s r c) -> p s r c", r=8, c=8)[:, :, :, v]
                            dve.wait_ge(qk_done, half * 16 + n + 1)
                            src = banks[4 + n % 4][64:128, :].rearrange("p (s c) -> p s c", c=8)
                            dve.tensor_scalar(dst, src, SCALE if qk == 0 else 1.0, rbias[64:128, qk, v:v + 1],
                                              ALU.mult, ALU.add).then_inc(q_right, 1)
                        if half == 0:
                            dve.wait_ge(wdt_turned, 1)
                            dve.tensor_copy(wd_t[:, :], banks[0][0:RANK, 0:P]).then_inc(wdt_copied, 1)
                    dve.wait_ge(wd_done, 1)
                    dve.wait_ge(wd_zeroed, 1)
                    for b in range(2):
                        q = slice(64 * b, 64 * b + 64)
                        dve.tensor_copy(w_delta[q, q], banks[1][q, 0:C]).then_inc(wd_copied, 1)
                    dve.wait_ge(a_done, 1)
                    dve.tensor_scalar(a_neg[:, :], a_neg[:, :], -1.0, None, ALU.mult).then_inc(a_done, 1)

        attention(nc, dict(kc=kc, h_all=h_all, xT=xT, qT=qT, kT=kT, w_v=w_v, w_proj=w_proj,
                           pb_row=pb_row, bv_col=bv_col, banks=banks, u_all=u_all))

        scan_and_experts(nc, dict(kc=kc, psum=psum, h_all=h_all, u=u_all, y=big_b, du=big_a, later=big_c,
                                  spare=(w_v, w_proj), w_delta=w_delta, wd=wd, b_col=b_col, d_col=d_col,
                                  a_neg=a_neg),
                         (router_w, router_b, w1, b1, w2, b2), out)


def attention(nc, t):
    kc, h_all, xT, qT, kT, u_all, banks = (t[n] for n in ("kc", "h_all", "xT", "qT", "kT", "u_all", "banks"))
    w_v, w_proj, pb_row, bv_col = (t[n] for n in ("w_v", "w_proj", "pb_row", "bv_col"))
    ident = kc[:, K_IDENT:K_IDENT + P]
    with ExitStack() as ctx:
        def sb(name, shape, dt=F32):
            return ctx.enter_context(nc.sbuf_tensor(name, shape, dt))

        def sem(name):
            return ctx.enter_context(nc.semaphore(name))

        q_st = sb("q_st", [P, 4, 2, WIN])
        k_st = sb("k_st", [P, 4, NH, WIN])
        x_st = sb("x_st", [P, 4, 2, WIN])
        top = sb("top", [P, 2, NH])
        low = sb("low", [P, 2, NH, WIN])
        prob = sb("prob", [P, 2, NH * WIN])
        prob_t = sb("prob_t", [P, 2, 512])
        v_st = sb("v_st", [P, 4, 2, 4, 2, HD + 1])
        inv = sb("inv", [P, 2, 2 * 4 * 2])
        o_st = sb("o_st", [P, 4, C])
        o_t = sb("o_t", [P, 2, P])
        nsum = sb("nsum", [P, 4])
        xc = sb("xc", [P, 4, C])
        sq = sb("sq", [P, 4, C])
        ssum = sb("ssum", [P, 4])
        var = sb("var", [P, 4])
        mhalf = sb("mhalf", [P, 4])
        rstd = sb("rstd", [P, 4])
        xh = sb("xh", [P, 4, C])

        q_masked, power_set, v_zeroed, ones_set = sem("q_masked"), sem("power_set"), sem("v_zeroed"), sem("ones_set")
        x_staged, k_masked, scores_done = sem("x_staged"), sem("k_masked"), sem("scores_done")
        top_done, low_done, prob_done = sem("top_done"), sem("low_done"), sem("prob_done")
        turned, prob_t_done, pv_done = sem("turned"), sem("prob_t_done"), sem("pv_done")
        v_done, v_copied = sem("v_done"), sem("v_copied")
        inv_done, o_done, ot_done, ot_copied = sem("inv_done"), sem("o_done"), sem("ot_done"), sem("ot_copied")
        proj_done, h_done, nsum_done, xc_done = sem("proj_done"), sem("h_done"), sem("nsum_done"), sem("xc_done")
        sq_done, ssum_done, var_done = sem("sq_done"), sem("ssum_done"), sem("var_done")
        rstd_done, xh_done = sem("rstd_done"), sem("xh_done")
        u_turned, u_copied = sem("u_turned"), sem("u_copied")

        LAST = QUADS + 4

        def steps(eng, body):
            for i in range(5):
                body(i)
            with eng.Fori(5, QUADS) as i:
                body(i)
            for i in range(QUADS, LAST + 1):
                body(i)

        def live(i, lag):
            return not isinstance(i, int) or 0 <= i - lag < QUADS

        def first(i, lag=0):
            return isinstance(i, int) and i - lag <= 0

        with nc.Block() as block:
            @block.sync
            def _(sp):
                def body(i):
                    if not first(i):
                        sp.wait_ge(v_done, i)
                    for d in range(2):
                        for k in range(2):
                            sp.dma_start(x_st[:, 2 * k:2 * k + 2, d, :], slot_pair(xT, i, k)).then_inc(x_staged, 16)

                body(0)
                with sp.Fori(1, QUADS) as i:
                    body(i)

            @block.gpsimd
            def _(pool):
                pool.memset(mhalf[:, :], -0.5).then_inc(power_set, 1)
                pool.wait_ge(power_set, 1)
                mask = kc[:, K_HEAD:K_HEAD + NH].unsqueeze(2).broadcast_to([P, NH, WIN])

                of_window = kc[:, K_WIN:K_WIN + 2].unsqueeze(1).unsqueeze(3).broadcast_to([P, 2, 2, WIN])

                def mask_q(i, k):
                    if not first(i):
                        pool.wait_ge(scores_done, i * 4 + (2 * k - 2))
                    q = slot_pair(qT, i, k).unsqueeze(2).broadcast_to([P, 2, 2, WIN])
                    pool.tensor_tensor(q_st[:, 2 * k:2 * k + 2], q, of_window, ALU.mult).then_inc(q_masked, 1)

                def mask_k(i, s):
                    if not first(i):
                        pool.wait_ge(scores_done, i * 4 + (s - 3))
                    k = slot_pair(kT, i, s // 2)[:, s % 2, :].unsqueeze(1).broadcast_to([P, NH, WIN])
                    pool.tensor_tensor(k_st[:, s], k, mask, ALU.mult).then_inc(k_masked, 1)

                def body(i):
                    if live(i, 0):
                        mask_k(i, 0)
                        mask_q(i, 0)
                        mask_k(i, 1)
                    if live(i, 4):
                        pool.wait_ge(xc_done, i - 3)
                        pool.tensor_tensor(sq[:, :, :], xc[:, :, :], xc[:, :, :], ALU.mult).then_inc(sq_done, 1)
                    if live(i, 0):
                        mask_k(i, 2)
                        mask_q(i, 1)
                    if live(i, 4):
                        pool.wait_ge(var_done, i - 3)
                        pool.tensor_tensor(rstd[:, :], var[:, :], mhalf[:, :], ALU.pow).then_inc(rstd_done, 1)
                        pool.wait_ge(rstd_done, i - 3)
                        if not first(i, 4):
                            pool.wait_ge(u_turned, i - 4)
                        pool.tensor_tensor(xh[:, :, :], xc[:, :, :],
                                           rstd[:, :].unsqueeze(2).broadcast_to([P, 4, C]), ALU.mult
                                           ).then_inc(xh_done, 1)
                    if live(i, 0):
                        mask_k(i, 3)

                steps(pool, body)

            @block.tensor
            def _(pe):
                pe.wait_ge(ones_set, 2)

                def scores(i, s):
                    pe.wait_ge(k_masked, i * 4 + (s + 1))
                    pe.wait_ge(q_masked, i * 2 + (s // 2 + 1))
                    if not (first(i) and s < 2):
                        pe.wait_ge(low_done, i * 4 + (s - 1))
                    pe.matmul(banks[s % 2][:, :], q_st[:, s], k_st[:, s], start=True, stop=True
                              ).then_inc(scores_done, 1)

                def turn(i, s):
                    pe.wait_ge(prob_done, i * 4 + (s + 1))
                    if not (first(i) and s < 2):
                        pe.wait_ge(prob_t_done, i * 4 + (s - 1))
                    for n in range(4):
                        m = pe.transpose(banks[2 + s % 2][:, n * P:n * P + P],
                                         prob[:, s % 2, n * P:n * P + P], ident)
                    m.then_inc(turned, 1)

                def products(i, s):
                    pe.wait_ge(prob_t_done, i * 4 + (s + 1))
                    pe.wait_ge(v_copied, i * 2 + (s // 2 + 1))
                    if s % 2 == 0 and not first(i):
                        pe.wait_ge(o_done, i * 2 + (s // 2 - 1))
                    o = banks[4 + s // 2][:, (s % 2) * 144:(s % 2) * 144 + 144]
                    for n in range(4):
                        m = pe.matmul(o[:, n * 36:n * 36 + 36], prob_t[:, s % 2, n * P:n * P + P],
                                      v_st[:, s, :, n, :, :], start=(s % 2 == 0 and n == 0), stop=True,
                                      skip_group_check=True)
                    m.then_inc(pv_done, 1)

                def body(i):
                    if live(i, 0):
                        scores(i, 0)
                    if live(i, 1):
                        turn(i - 1, 2)
                        products(i - 1, 1)
                    if live(i, 2):
                        pe.wait_ge(o_done, i * 2 - 2)
                        if not first(i, 2):
                            pe.wait_ge(h_done, i - 2)
                        for n in range(2):
                            m = pe.transpose(banks[7][:, n * P:n * P + P], o_st[:, 2 * n:2 * n + 2, :], ident)
                        m.then_inc(ot_done, 1)
                    if live(i, 0):
                        pe.wait_ge(x_staged, (i + 1) * 64)
                        if not first(i):
                            pe.wait_ge(v_copied, i * 2)
                        for s in range(4):
                            m = pe.matmul(banks[6][:, s * P:s * P + P], x_st[:, s], w_v[:, :],
                                          start=True, stop=True, skip_group_check=True)
                        m.then_inc(v_done, 1)
                        scores(i, 1)
                    if live(i, 1):
                        turn(i - 1, 3)
                        products(i - 1, 2)
                    if live(i, 4):
                        pe.wait_ge(xh_done, i - 3)
                        if live(i, 2):
                            pe.wait_ge(ot_copied, i - 1)
                        else:
                            pe.wait_ge(h_done, QUADS)
                            pe.wait_ge(u_copied, i - 4)
                        for n in range(2):
                            m = pe.transpose(banks[7][:, n * P:n * P + P], xh[:, 2 * n:2 * n + 2, :], ident)
                        m.then_inc(u_turned, 1)
                    if live(i, 0):
                        scores(i, 2)
                        turn(i, 0)
                    if live(i, 1):
                        products(i - 1, 3)
                    if live(i, 0):
                        scores(i, 3)
                        turn(i, 1)
                        products(i, 0)
                    if live(i, 2):
                        pe.wait_ge(ot_copied, i - 1)
                        if live(i, 4):
                            pe.wait_ge(u_copied, i - 3)
                        for n in range(2):
                            m = pe.matmul(banks[7][:, 256 + n * P:256 + n * P + P], o_t[:, n, :], w_proj[:, :],
                                          start=(n == 0), stop=True, skip_group_check=True)
                        m.then_inc(proj_done, 1)

                steps(pe, body)

            @block.scalar
            def _(act):
                act.wait_ge(ones_set, 2)

                def exps(i, s):
                    act.wait_ge(low_done, i * 4 + (s + 1))
                    if not (first(i) and s < 2):
                        act.wait_ge(turned, i * 4 + (s - 1))
                    act.activation(prob[:, s % 2, :], low[:, s % 2], ACT.Exp).then_inc(prob_done, 1)

                def copy_t(i, s):
                    act.wait_ge(turned, i * 4 + (s + 1))
                    if not (first(i) and s < 2):
                        act.wait_ge(pv_done, i * 4 + (s - 1))
                    act.activation(prob_t[:, s % 2, :], banks[2 + s % 2][:, :], ACT.Copy).then_inc(prob_t_done, 1)

                def copy_v(i, hf):
                    act.wait_ge(v_done, i + 1)
                    if not first(i):
                        act.wait_ge(pv_done, i * 4 + (2 * hf - 2))
                    for e in range(2):
                        q = slice(64 * e, 64 * e + 64)
                        src = banks[6][q, hf * 256:hf * 256 + 256].rearrange(
                            "p (sw n e d) -> p sw n e d", n=4, e=2, d=HD)[:, :, :, e, :]
                        dst = v_st[q, 2 * hf:2 * hf + 2, :, :, e, 0:HD].rearrange("p s w n d -> p (s w) n d")
                        a = act.activation(dst, src, ACT.Copy)
                    a.then_inc(v_copied, 1)

                def body(i):
                    if live(i, 1):
                        copy_t(i - 1, 2)
                    if live(i, 0):
                        exps(i, 0)
                    if live(i, 2):
                        act.wait_ge(ot_done, i - 1)
                        if not first(i, 2):
                            act.wait_ge(proj_done, i - 2)
                        for n in range(2):
                            a = act.activation(o_t[:, n, :].rearrange("p (r w c) -> p w r c", w=2, r=8),
                                               banks[7][:, n * P:n * P + P].rearrange("p (w r c) -> p w r c", w=2, r=8),
                                               ACT.Identity, bias=bv_col[:, 0:1])
                        a.then_inc(ot_copied, 1)
                    if live(i, 1):
                        copy_t(i - 1, 3)
                    if live(i, 0):
                        copy_v(i, 0)
                        exps(i, 1)
                    if live(i, 4):
                        act.wait_ge(u_turned, i - 3)
                        j = i - 4
                        at = j // 2 * 512 + j % 2 * 32
                        a = act.activation(raster(u_all, at), banks[7][:, 0:256].rearrange(
                            "p (k r x) -> p k r x", k=2, r=8), ACT.Copy)
                        a.then_inc(u_copied, 1)
                    if live(i, 0):
                        copy_t(i, 0)
                        exps(i, 2)
                        copy_t(i, 1)
                        exps(i, 3)
                        copy_v(i, 1)

                steps(act, body)

            @block.vector
            def _(dve):
                ones = v_st[:, :, :, :, :, HD]
                dve.memset(v_st[:, :, :, :, :, :], 0.0).then_inc(v_zeroed, 1)
                dve.wait_ge(v_zeroed, 1)
                for e in range(2):
                    q = slice(64 * e, 64 * e + 64)
                    dve.memset(v_st[q, :, :, :, e, HD:HD + 1].rearrange("p s w n o -> p (s w) n o"), 1.0
                               ).then_inc(ones_set, 1)

                def lower(i, s):
                    sc = banks[s % 2][:, :].rearrange("p (h k) -> p h k", h=NH)
                    dve.wait_ge(scores_done, i * 4 + (s + 1))
                    dve.tensor_reduce(top[:, s % 2, :], sc, AX.X, ALU.max).then_inc(top_done, 1)
                    dve.wait_ge(top_done, i * 4 + (s + 1))
                    if not (first(i) and s < 2):
                        dve.wait_ge(prob_done, i * 4 + (s - 1))
                    dve.tensor_tensor(low[:, s % 2], sc,
                                      top[:, s % 2, :].unsqueeze(2).broadcast_to([P, NH, WIN]),
                                      ALU.subtract).then_inc(low_done, 1)

                def normalise(i, hf):
                    dve.wait_ge(pv_done, i * 4 + (2 * hf + 2))
                    if not first(i):
                        dve.wait_ge(ot_done, i)
                    o = banks[4 + hf][:, 0:288].rearrange("p (sn w e d) -> p sn w e d", sn=8, w=2, e=2)
                    for w in range(2):
                        q = slice(64 * w, 64 * w + 64)
                        dve.reciprocal(inv[q, hf, :].rearrange("p (sn e) -> p sn e", e=2),
                                       o[q, :, w, :, HD]).then_inc(inv_done, 1)
                    dve.wait_ge(inv_done, i * 4 + (2 * hf + 2))
                    for w in range(2):
                        q = slice(64 * w, 64 * w + 64)
                        m = dve.tensor_tensor(
                            o_st[q, 2 * hf:2 * hf + 2, :].rearrange("p s (n e d) -> p (s n) e d", n=4, e=2),
                            o[q, :, w, :, 0:HD],
                            inv[q, hf, :].rearrange("p (sn e) -> p sn e", e=2).unsqueeze(3).broadcast_to([64, 8, 2, HD]),
                            ALU.mult)
                    m.then_inc(o_done, 1)

                def body(i):
                    if live(i, 0):
                        lower(i, 0)
                    if live(i, 3):
                        h = h_all[:, bass.ds(i * 4 - 12, 4), :]
                        dve.tensor_reduce(nsum[:, :], h, AX.X, ALU.add, negate=True).then_inc(nsum_done, 1)
                        dve.wait_ge(nsum_done, i - 2)
                        if not first(i, 3):
                            dve.wait_ge(xh_done, i - 3)
                        dve.scalar_tensor_tensor(xc[:, :, :], nsum[:, :].unsqueeze(2).broadcast_to([P, 4, C]),
                                                 1.0 / C, h, ALU.mult, ALU.add).then_inc(xc_done, 1)
                    if live(i, 0):
                        lower(i, 1)
                    if live(i, 1):
                        normalise(i - 1, 0)
                    if live(i, 0):
                        lower(i, 2)
                    if live(i, 3):
                        dve.wait_ge(sq_done, i - 2)
                        dve.tensor_reduce(ssum[:, :], sq[:, :, :], AX.X, ALU.add).then_inc(ssum_done, 1)
                        dve.wait_ge(ssum_done, i - 2)
                        dve.tensor_scalar(var[:, :], ssum[:, :], 1.0 / C, LN_EPS, ALU.mult, ALU.add
                                          ).then_inc(var_done, 1)
                    if live(i, 0):
                        lower(i, 3)
                    if live(i, 1):
                        normalise(i - 1, 1)
                    if live(i, 2):
                        dve.wait_ge(proj_done, i - 1)
                        dve.tensor_tensor(h_all[:, bass.ds(i * 4 - 8, 4), :],
                                          banks[7][:, 256:512].rearrange("p (s d) -> p s d", s=4),
                                          pb_row[:, :].unsqueeze(1).broadcast_to([P, 4, C]), ALU.add
                                          ).then_inc(h_done, 1)
                        dve.wait_ge(h_done, i - 1)

                steps(dve, body)


def slot_pair(arr, i, k):
    a = arr[:, bass.ds(i * (2 * WIN) + i // 16 * (L // 2) + k * WIN, L // 2 + WIN)]
    return bass.AP(tensor=a.tensor, offset=a.offset, ap=[list(a.ap[0]), [L // 2, 2], [1, WIN]],
                   dep_tracking_offset=a.dep_tracking_offset)


def raster(arr, at):
    a = arr[:, bass.ds(at, 7 * SIDE + 32)]
    return bass.AP(tensor=a.tensor, offset=a.offset, ap=[list(a.ap[0]), [16, 2], [SIDE, 8], [1, 16]],
                   dep_tracking_offset=a.dep_tracking_offset)


def scan_and_experts(nc, t, moe, out):
    with ExitStack() as ctx:
        def sb(name, shape, dt=F32):
            return ctx.enter_context(nc.sbuf_tensor(name, shape, dt))

        t["w1x"] = sb("w1x", [P, NE, HID])
        t["w2x"] = sb("w2x", [P, 4, C])
        t["b2x"] = sb("b2x", [P, 2, C])
        t["rw"] = sb("rw", [NE, C])
        t["rwx"] = sb("rwx", [C, NE])
        t["rb_row"] = sb("rb_row", [P, NE])
        with ExitStack() as scan_ctx:
            selective_scan(nc, scan_ctx, t, moe)
        experts(nc, ctx, t, out)


def selective_scan(nc, ctx, t, moe):
    router_w, router_b, w1, b1, w2, b2 = moe
    w1x, w2x, b2x, rwx, rb_row, rw = (t[n] for n in ("w1x", "w2x", "b2x", "rwx", "rb_row", "rw"))
    kc, psum, u, y, du, later, w_delta, wd, b_col, d_col, a_neg = (
        t[n] for n in ("kc", "psum", "u", "y", "du", "later", "w_delta", "wd", "b_col", "d_col", "a_neg"))

    def sb(name, shape, dt=F32):
        return ctx.enter_context(nc.sbuf_tensor(name, shape, dt))

    def sem(name):
        return ctx.enter_context(nc.semaphore(name))

    STEP = 1024
    CH = HALVES * L // STEP
    ones = sb("ones", [P, 1])
    eps = sb("eps", [P, 1])
    rmin = sb("rmin", [P, 2])
    alive = sb("alive", [P, 2 * NS])
    alive_n = sb("alive_n", [1, 2 * NS + 1], I32)
    carry = sb("carry", [P, HALVES, NS])
    bufs = sb("bufs", [P, 3, 4 * BLK])
    buf_a, buf_b, buf_c = (bufs[:, i, :] for i in range(3))
    tail_a = sb("tail_a", [P, NS * P])
    tail_b = sb("tail_b", [P, NS * P])
    mag = tail_a[:, :].rearrange("p (a b) -> p a b", a=2)

    const_set, pos_done, z_done, z_read = sem("const_set"), sem("pos_done"), sem("z_done"), sem("z_read")
    e_done, ln_done, delta_done, scan_done = sem("e_done"), sem("ln_done"), sem("delta_done"), sem("scan_done")
    last_set, y_set, du_done = sem("last_set"), sem("y_set"), sem("du_done")
    rmin_done, alive_done, count_done, flag_done = sem("rmin_done"), sem("alive_done"), sem("count_done"), sem("flag_done")
    tail_cum, tail_ln, tail_rec, eps_set = sem("tail_cum"), sem("tail_ln"), sem("tail_rec"), sem("eps_set")
    u_tail, later_tail, du_tail, y_tail = (
        buf[:, :].rearrange("p (a t) -> p a t", a=2)[:, :, L - TAIL:L] for buf in (u, later, du, y))
    moe_in, b2_set, rw_turned = sem("moe_in"), sem("b2_set"), sem("rw_turned")

    with nc.Block() as block:
        @block.sync
        def _(sp):
            sp.dma_start(w1x[0:C, :, :], w1.rearrange("e d h -> d e h")).then_inc(moe_in, 16)
            sp.dma_start(w1x[96:P, :, :], b1.partition_broadcast(NE)).then_inc(moe_in, 16)
            sp.dma_start(w2x[:, :, :], w2.rearrange("(g e) h d -> (e h) g d", g=4)).then_inc(moe_in, 16)
            sp.dma_start(rw[:, :], router_w).then_inc(moe_in, 16)
            sp.dma_start(rb_row[:, :], router_b.partition_broadcast(P)).then_inc(moe_in, 16)
            sp.wait_ge(b2_set, 2)
            for g in range(4):
                sp.dma_start(b2x[96 + 8 * g:104 + 8 * g, g % 2, :], b2[8 * g:8 * g + 8, :]).then_inc(moe_in, 16)
            sp.wait_ge(moe_in, 16 * 9)

        @block.tensor
        def _(pe):
            for n in range(CH):
                if n >= 2:
                    pe.wait_ge(z_read, n - 1)
                for k in range(2):
                    m = pe.matmul(psum[:, n % 2 * 2 + k, :], w_delta[:, :],
                                  u[:, n * STEP + k * 512:n * STEP + k * 512 + 512], start=True, stop=True)
                m.then_inc(z_done, 1)
            pe.wait_ge(const_set, 1)
            pe.wait_ge(moe_in, 16 * 9)
            pe.transpose(psum[0:C, 6, 0:NE], rw[:, :], kc[0:NE, 0:NE]).then_inc(rw_turned, 1)
            pe.wait_ge(alive_done, 2)
            pe.matmul(psum[0:1, 7, 0:2 * NS], ones[:, :], alive[:, :], start=True, stop=True).then_inc(count_done, 1)

        @block.vector
        def _(dve):
            def later_sum(half):
                dve.wait_ge(delta_done, (half + 1) * CH // 2)
                dve.wait_ge(last_set, half + 1)
                at = half * L
                dve.tensor_tensor_scan(backwards(later, at, L - 1), ones[:, 0:1].to_broadcast([P, L - 1]),
                                       backwards(du, at + 1, L - 1), 0.0, ALU.mult, ALU.add).then_inc(scan_done, 1)

            dve.wait_ge(const_set, 1)
            for n in range(CH):
                dve.wait_ge(z_done, n + 1)
                z = psum[:, n % 2 * 2:n % 2 * 2 + 2, :].rearrange("p b n -> p (b n)")
                m = slice(n * STEP, n * STEP + STEP)
                dve.tensor_scalar(du[:, m], z, b_col[:, 0:1], 0.0, ALU.add, ALU.max).then_inc(pos_done, 1)
                dve.wait_ge(pos_done, n + 1)
                if n >= 2:
                    dve.wait_ge(e_done, n - 1)
                dve.scalar_tensor_tensor(mag[:, n % 2, :], du[:, m], -2.0, z, ALU.mult, ALU.add).then_inc(z_read, 1)
            eye = kc[:, K_EYE:K_EYE + NE].unsqueeze(2).to_broadcast([P, NE, HID])
            dve.wait_ge(moe_in, 16 * 9)
            dve.tensor_scalar(w1x[64:96, :, :], eye[64:96], -BIG, None, ALU.mult)
            dve.tensor_tensor(w1x[96:P, :, :], w1x[96:P, :, :], eye[96:P], ALU.mult)
            dve.wait_ge(rw_turned, 1)
            dve.tensor_copy(rwx[:, :], psum[0:C, 6, 0:NE])
            later_sum(0)
            later_sum(1)
            dve.wait_ge(scan_done, 2)
            for m, last in enumerate((L - TAIL - BLK - 1, L - TAIL - 1)):
                dve.tensor_tensor(rmin[:, m:m + 1], later[:, last:last + 1], later[:, L + last:L + last + 1],
                                  ALU.min).then_inc(rmin_done, 1)
            dve.wait_ge(rmin_done, 2)
            for m in range(2):
                dve.tensor_scalar(alive[:, m * NS:m * NS + NS], a_neg[:, :], rmin[:, m:m + 1], EXP_ZERO,
                                  ALU.mult, ALU.is_gt).then_inc(alive_done, 1)
            at = L
            dve.tensor_tensor(du[:, at:at + L], du[:, at:at + L], u[:, at:at + L], ALU.mult).then_inc(du_done, 1)
            m = slice(3 * 2048, 4 * 2048)
            dve.tensor_scalar(y[:, m], u[:, m], d_col[:, 0:1], None, ALU.mult).then_inc(y_set, 1)
            dve.wait_ge(count_done, 1)
            dve.tensor_copy(alive_n[:, 0:2 * NS], psum[0:1, 7, 0:2 * NS]).then_inc(flag_done, 1)
            dve.tensor_reduce(alive_n[:, 2 * NS:2 * NS + 1], psum[0:1, 7, NS + SLOW:2 * NS], AX.X, ALU.max
                              ).then_inc(flag_done, 1)

        @block.scalar
        def _(act):
            for n in range(CH):
                act.wait_ge(z_read, n + 1)
                m = slice(n * STEP, n * STEP + STEP)
                act.activation(later[:, m], mag[:, n % 2, :], ACT.Exp, bias=b_col[:, 0:1]).then_inc(e_done, 1)
                act.wait_ge(e_done, n + 1)
                act.activation(later[:, m], later[:, m], ACT.Ln, bias=1.0).then_inc(ln_done, 1)
            for n in range(3):
                m = slice(n * 2048, n * 2048 + 2048)
                act.activation(y[:, m], u[:, m], ACT.Copy, scale=d_col[:, 0:1]).then_inc(y_set, 1)
            act.wait_ge(scan_done, 2)
            act.wait_ge(z_read, CH)
            for n in range(NS):
                e = act.activation(tail_a[:, n * P:n * P + P].rearrange("p (a t) -> p a t", a=2), later_tail,
                                   ACT.Exp, scale=a_neg[:, n:n + 1])
            e.then_inc(tail_cum, 1)
            act.wait_ge(tail_cum, 1)
            act.wait_ge(eps_set, 1)
            act.activation(tail_b[:, :], tail_a[:, :], ACT.Ln, bias=eps[:, 0:1]).then_inc(tail_ln, 1)
            act.wait_ge(tail_ln, 1)
            act.activation(tail_b[:, :], tail_b[:, :], ACT.Exp, scale=-1.0).then_inc(tail_rec, 1)

        @block.gpsimd
        def _(pool):
            pool.memset(b2x[:, :, :], 0.0).then_inc(b2_set, 1)
            pool.wait_ge(b2_set, 1)
            pool.memset(b2x[96:P, :, :], -BIG).then_inc(b2_set, 1)
            pool.wait_ge(b2_set, 2)
            pool.memset(ones[:, :], 1.0).then_inc(const_set, 1)
            pool.memset(eps[:, :], SCAN_EPS).then_inc(eps_set, 1)
            pool.memset(carry[:, :, :], 0.0)
            for n in range(CH):
                pool.wait_ge(ln_done, n + 1)
                m = slice(n * STEP, n * STEP + STEP)
                pool.tensor_tensor(du[:, m], du[:, m], later[:, m], ALU.add).then_inc(delta_done, 1)
                if (n + 1) % (CH // 2) == 0:
                    pool.wait_ge(delta_done, n + 1)
                    pool.memset(later[:, n * STEP + STEP - 1:n * STEP + STEP], 0.0).then_inc(last_set, 1)
            pool.wait_ge(scan_done, 1)
            pool.tensor_tensor(du[:, 0:L], du[:, 0:L], u[:, 0:L], ALU.mult).then_inc(du_done, 1)

    rep_staged, b_done, c_done, cum_done, lnc_done, rec_done = (
        sem("rep_staged"), sem("b_done"), sem("c_done"), sem("cum_done"), sem("lnc_done"), sem("rec_done"))
    duc_done, term_done, sum_done, ratio_done, out_done, y_added, state_set, state_kept = (
        sem("duc_done"), sem("term_done"), sem("sum_done"), sem("ratio_done"), sem("out_done"),
        sem("y_added"), sem("state_set"), sem("state_kept"))
    rep_made, tail_du, tail_bc, tail_term, tail_sum, tail_out = (
        sem("rep_made"), sem("tail_du"), sem("tail_bc"), sem("tail_term"),
        sem("tail_sum"), sem("tail_out"))
    w_b, w_c = t["spare"]
    w_rep = later[:, 0:L].rearrange("p (n d) -> p n d", d=P)
    a_n = sb("a_n", [P, 1])
    state = sb("state", [P, HALVES])
    CR = 2
    credited = (c_done, rec_done, term_done, ratio_done, out_done, y_added)

    def two(buf, r):
        return buf[:, r * 2 * BLK:(r + 1) * 2 * BLK].rearrange("p (a t) -> p a t", a=2)

    def block_of(arr, blk):
        if isinstance(blk, int):
            return arr[:, :].rearrange("p (a t) -> p a t", a=2)[:, :, blk * BLK:blk * BLK + BLK]
        return arr[:, :].rearrange("p (a t) -> p a t", a=2)[:, :, bass.ds(blk * BLK, BLK)]

    def states(eng, mine, last, start, far, near, end, between):
        credit = CR if last in credited else 0
        for s in mine:
            if s in credited:
                eng.sem_inc(s, CR)

        def skip(q, n):
            if not (isinstance(q, int) and credit + q == 0):
                eng.wait_ge(last, q + credit)
            for s in mine:
                eng.sem_inc(s, n)

        def some(lo, hi):
            with eng.Fori(lo, hi) as n:
                is_near = eng.value_load(alive_n[0:1, bass.ds(n + NS, 1)], min_val=0, max_val=P)
                start(n)
                is_far = eng.value_load(alive_n[0:1, bass.ds(n, 1)], min_val=0, max_val=P)
                with eng.If(is_far > 0):
                    far(n * BLOCKS)
                with eng.Else():
                    skip(n * BLOCKS, BLOCKS - 1)
                with eng.If(is_near > 0):
                    near(n * BLOCKS)
                with eng.Else():
                    skip(n * BLOCKS + (BLOCKS - 1), 1)
                end(n)

        some(0, SLOW)
        between()
        rest = eng.value_load(alive_n[0:1, 2 * NS:2 * NS + 1], min_val=0, max_val=P)
        with eng.If(rest > 0):
            some(SLOW, NS)
        with eng.Else():
            skip(SLOW * BLOCKS, (NS - SLOW) * BLOCKS)

    def nothing(*_):
        pass

    def far_near(eng, body):
        def far(q0):
            with eng.Fori(0, (BLOCKS - 1) // 2) as pair:
                for r in range(2):
                    body(q0 + pair * 2 + r, pair * 2 + r, r)

        def near(q0):
            body(q0 + (BLOCKS - 1), BLOCKS - 1, 0)
        return far, near

    with nc.Block() as block:
        @block.gpsimd
        def _(pool):
            def duc(q, blk, r):
                pool.wait_ge(lnc_done, q + 1)
                pool.tensor_tensor(two(buf_a, r), two(buf_a, r), block_of(du, blk), ALU.mult).then_inc(duc_done, 1)

            def add(q, blk, r):
                pool.wait_ge(out_done, q + (CR + 1))
                pool.tensor_tensor(block_of(y, blk), block_of(y, blk), two(buf_c, r), ALU.add).then_inc(y_added, 1)

            def start(n):
                pool.wait_ge(c_done, n * BLOCKS + CR)
                pool.wait_ge(rec_done, n * BLOCKS + CR)
                pool.wait_ge(out_done, n * BLOCKS + CR)
                pool.wait_ge(y_added, n * BLOCKS + CR)
                pool.tensor_copy(a_n[:, :], a_neg[:, bass.ds(n, 1)]).then_inc(rep_staged, 1)
                pool.wait_ge(rep_staged, n * 5 + 1)
                for w, at in ((w_b, RANK), (w_c, RANK + NS)):
                    for b in range(2):
                        q = slice(64 * b, 64 * b + 64)
                        pool.tensor_copy(w[q, q], wd[q, bass.ds(n + at, 1)].to_broadcast([64, 64])
                                         ).then_inc(rep_staged, 1)
                pool.wait_ge(rep_staged, n * 5 + 5)

            def far(q0):
                duc(q0, 0, 0)
                with pool.Fori(0, (BLOCKS - 1) // 2 - 1) as pair:
                    for r in range(2):
                        duc(q0 + pair * 2 + (r + 1), pair * 2 + (r + 1), 1 - r)
                        add(q0 + pair * 2 + r, pair * 2 + r, r)
                m = BLOCKS - 2
                duc(q0 + m, m, m % 2)
                add(q0 + (m - 1), m - 1, (m - 1) % 2)
                add(q0 + m, m, m % 2)

            def near(q0):
                duc(q0 + (BLOCKS - 1), BLOCKS - 1, 0)
                add(q0 + (BLOCKS - 1), BLOCKS - 1, 0)

            states(pool, (duc_done, y_added), y_added, start, far, near, nothing, nothing)

        @block.tensor
        def _(pe):
            def body(q, blk, r):
                for k, w, used, done in ((0, w_b, term_done, b_done), (2, w_c, out_done, c_done)):
                    pe.wait_ge(used, q + (CR - 1))
                    for half in range(HALVES):
                        m = pe.matmul(psum[:, 4 * r + k + half, 0:BLK], w[:, :],
                                      u[:, bass.ds(half * L + blk * BLK, BLK)], start=True, stop=True)
                    m.then_inc(done, 1)

            def start(n):
                pe.wait_ge(rep_staged, n * 5 + 5)

            states(pe, (b_done, c_done), c_done, start, *far_near(pe, body), nothing, nothing)
            pe.wait_ge(rep_made, 4)
            pe.wait_ge(out_done, NS * BLOCKS + CR)
            for n in range(2 * NS):
                m = pe.matmul(psum[:, n // 4, n % 4 * P:n % 4 * P + P], w_rep[:, n, :], u_tail,
                              start=True, stop=True, skip_group_check=True)
                if n % 8 == 7:
                    m.then_inc(tail_bc, 1)

        @block.scalar
        def _(act):
            def body(q, blk, r):
                act.wait_ge(ratio_done, q + (CR - 1))
                act.activation(two(buf_a, r), block_of(later, blk), ACT.Exp, scale=a_n[:, 0:1]).then_inc(cum_done, 1)
                act.wait_ge(cum_done, q + 1)
                act.activation(two(buf_b, r), two(buf_a, r), ACT.Ln, bias=eps[:, 0:1]).then_inc(lnc_done, 1)
                act.wait_ge(lnc_done, q + 1)
                act.activation(two(buf_b, r), two(buf_b, r), ACT.Exp, scale=-1.0).then_inc(rec_done, 1)

            def start(n):
                act.wait_ge(rep_staged, n * 5 + 1)

            states(act, (cum_done, lnc_done, rec_done), rec_done, start, *far_near(act, body), nothing, nothing)
            for b in range(2):
                q, other = slice(64 * b, 64 * b + 64), slice(64 - 64 * b, 128 - 64 * b)
                act.activation(w_rep[q, :, q], wd[q, RANK:].unsqueeze(2).to_broadcast([64, 2 * NS, 64]), ACT.Copy
                               ).then_inc(rep_made, 1)
                act.activation(w_rep[q, :, other], ones[q, :].unsqueeze(2).to_broadcast([64, 2 * NS, 64]), ACT.Copy,
                               scale=0.0).then_inc(rep_made, 1)

        @block.vector
        def _(dve):
            def body(q, blk, r):
                dve.wait_ge(b_done, q + 1)
                dve.wait_ge(duc_done, q + 1)
                a, c = two(buf_a, r), two(buf_c, r)
                dve.tensor_tensor(a, a, psum[:, 4 * r:4 * r + 2, 0:BLK], ALU.mult).then_inc(term_done, 1)
                dve.wait_ge(term_done, q + (CR + 1))
                dve.wait_ge(y_added, q + (CR - 1))
                for half in range(HALVES):
                    m = dve.tensor_tensor_scan(c[:, half, :], ones[:, 0:1].to_broadcast([P, BLK]), a[:, half, :],
                                               state[:, half:half + 1], ALU.mult, ALU.add)
                m.then_inc(sum_done, 1)
                dve.wait_ge(sum_done, q + 1)
                dve.tensor_copy(state[:, :], c[:, :, BLK - 1]).then_inc(state_set, 1)
                dve.wait_ge(rec_done, q + (CR + 1))
                dve.wait_ge(state_set, q + 1)
                dve.tensor_tensor(c, c, two(buf_b, r), ALU.mult).then_inc(ratio_done, 1)
                dve.wait_ge(ratio_done, q + (CR + 1))
                dve.wait_ge(c_done, q + (CR + 1))
                dve.tensor_tensor(c, c, psum[:, 4 * r + 2:4 * r + 4, 0:BLK], ALU.mult).then_inc(out_done, 1)

            def start(n):
                dve.memset(state[:, :], 0.0).then_inc(state_kept, 1)
                dve.wait_ge(state_kept, n * 2 + 1)

            def end(n):
                dve.tensor_copy(carry[:, :, bass.ds(n, 1)], state[:, :].unsqueeze(2)).then_inc(state_kept, 1)
                dve.wait_ge(state_kept, n * 2 + 2)

            all_n = tail_a[:, :].rearrange("p (n a t) -> p n a t", n=NS, a=2)

            def between():
                dve.tensor_tensor(all_n, all_n, du_tail.unsqueeze(1).broadcast_to([P, NS, 2, TAIL]), ALU.mult
                                  ).then_inc(tail_du, 1)

            states(dve, (term_done, sum_done, state_set, ratio_done, out_done), out_done,
                   start, *far_near(dve, body), end, between)
            dve.wait_ge(tail_du, 1)
            for m in range(2):
                k = slice(m * 1024, m * 1024 + 1024)
                dve.wait_ge(tail_bc, m + 1)
                dve.tensor_tensor(tail_a[:, k], tail_a[:, k], psum[:, 2 * m:2 * m + 2, :].rearrange("p b n -> p (b n)"),
                                  ALU.mult).then_inc(tail_term, 1)
            dve.wait_ge(tail_term, 2)
            dve.tensor_tensor(all_n[:, :, :, 0], all_n[:, :, :, 0], carry[:, :, :].rearrange("p a n -> p n a"),
                              ALU.add).then_inc(tail_term, 1)
            dve.wait_ge(tail_term, 3)
            sums = bufs[:, :, :].rearrange("p a n -> p (a n)")[:, 0:NS * P]
            for m in range(4):
                s = dve.tensor_tensor_scan(sums[:, m * 512:m * 512 + 512], kc[:, K_SEG:K_SEG + 512],
                                           tail_a[:, m * 512:m * 512 + 512], 0.0, ALU.mult, ALU.add)
                s.then_inc(tail_sum, 1)
            dve.wait_ge(tail_rec, 1)
            for m in range(2):
                k = slice(m * 1024, m * 1024 + 1024)
                dve.wait_ge(tail_sum, 2 * m + 2)
                dve.tensor_tensor(sums[:, k], sums[:, k], tail_b[:, k], ALU.mult).then_inc(tail_sum, 4)
            for m in range(2):
                k = slice(m * 1024, m * 1024 + 1024)
                dve.wait_ge(tail_sum, 12)
                dve.wait_ge(tail_bc, m + 3)
                dve.tensor_tensor(sums[:, k], sums[:, k], psum[:, 4 + 2 * m:6 + 2 * m, :].rearrange("p b n -> p (b n)"),
                                  ALU.mult).then_inc(tail_out, 1)
            dve.wait_ge(tail_out, 2)
            dve.tensor_reduce(tail_b[:, 0:P], sums.rearrange("p (n x) -> p x n", n=NS), AX.X, ALU.add
                              ).then_inc(tail_out, 1)
            dve.wait_ge(tail_out, 3)
            dve.tensor_tensor(y_tail, y_tail, tail_b[:, 0:P].rearrange("p (a t) -> p a t", a=2), ALU.add
                              ).then_inc(tail_out, 1)


def backwards(arr, at, n):
    ap = arr[:, at + n - 1:at + n]
    return bass.AP(tensor=ap.tensor, offset=ap.offset, ap=[list(ap.ap[0]), [-1, n]])


def store_quad(eng, out, src, i, done):
    at = i // 2 * 512 + i % 2 * 32 + i // 16 * L
    flat = out.rearrange("b t d -> (b t) d")
    for k in range(2):
        for b2 in range(2):
            a = flat[bass.ds(at + (k * 16 + b2 * L), 1), :]
            dst = bass.AP(tensor=a.tensor, offset=a.offset, ap=[[SIDE * C, 8], [C, 16], [1, C]],
                          dep_tracking_offset=a.dep_tracking_offset)
            eng.dma_start(dst, src[:, 2 * k + b2, :]).then_inc(done, 16)


def experts(nc, ctx, t, out):
    kc, psum, y, h_all, w1x, w2x, b2x, rwx, rb_row = (
        t[n] for n in ("kc", "psum", "y", "h_all", "w1x", "w2x", "b2x", "rwx", "rb_row"))
    ident = kc[:, K_IDENT:K_IDENT + P]

    def sb(name, shape, dt=F32):
        return ctx.enter_context(nc.sbuf_tensor(name, shape, dt))

    def sem(name):
        return ctx.enter_context(nc.semaphore(name))

    y_st = sb("y_st", [P, 2, P])
    h_seen = sb("h_seen", [P, 1])
    nsum = sb("m_nsum", [P, 4])
    xc = sb("m_xc", [P, 4, C])
    sq = sb("m_sq", [P, 4, C])
    ssum = sb("m_ssum", [P, 4])
    var = sb("m_var", [P, 4])
    mhalf = sb("m_mhalf", [P, 4])
    rstd = sb("m_rstd", [P, 4])
    xh = sb("m_xh", [P, 4, C])
    lg = sb("lg", [P, 4, NE])
    best = sb("best", [P, 4])
    rank = sb("rank", [P, 4, NE])
    best_rank = sb("best_rank", [P, 4])
    mark = sb("mark", [P, 4, 2, NE])
    comb_t = sb("comb_t", [P, 2, 4 * P])
    hid = sb("hid", [P, 2, 4 * P])
    best_o = sb("best_o", [P, 4, C])
    out_st = sb("out_st", [P, 4, C])

    power_set = sem("m_power_set")
    y_staged, y_turned, h_done = sem("y_staged"), sem("y_turned"), sem("m_h_done")
    nsum_done, xc_done, sq_done, ssum_done = sem("m_nsum_done"), sem("m_xc_done"), sem("m_sq_done"), sem("m_ssum_done")
    var_done, rstd_done, xh_done = sem("m_var_done"), sem("m_rstd_done"), sem("m_xh_done")
    x_turned, x_copied, logits_done, lg_done = sem("m_x_turned"), sem("m_x_copied"), sem("logits_done"), sem("lg_done")
    best_done, eq_done, rank_done, chosen = sem("best_done"), sem("eq_done"), sem("rank_done"), sem("chosen")
    mark_turned, mark_copied = sem("mark_turned"), sem("mark_copied")
    hid_done, relu_done, collapsed = sem("hid_done"), sem("relu_done"), sem("collapsed")
    o_done, picked, out_made, stored = sem("m_o_done"), sem("picked"), sem("out_made"), sem("stored")

    LAST = QUADS + 2
    HID_BANK = (4, 5, 7, 2)

    def steps(eng, body):
        for i in range(4):
            body(i, i % 2)
        with eng.Fori(2, QUADS // 2) as pair:
            for par in range(2):
                body(pair * 2 + par, par)
        for i in range(QUADS, LAST + 1):
            body(i, i % 2)

    def live(i, lag):
        return not isinstance(i, int) or 0 <= i - lag < QUADS

    def first(i, lag=0):
        return isinstance(i, int) and i - lag <= 0

    def by_slot(rows, par):
        return comb_t[rows, par, :].rearrange("p (k b q) -> p b k q", k=2, b=2)

    with nc.Block() as block:
        @block.sync
        def _(sp):
            with sp.Fori(0, QUADS) as i:
                sp.wait_ge(out_made, i + 1)
                store_quad(sp, out, out_st[:, :, :], i, stored)
            sp.wait_ge(stored, QUADS * 64)

        @block.gpsimd
        def _(pool):
            pool.memset(mhalf[:, :], -0.5).then_inc(power_set, 1)
            pool.wait_ge(power_set, 1)

            def body(i, par):
                if not live(i, 0):
                    return
                pool.wait_ge(xc_done, i + 1)
                pool.tensor_tensor(sq[:, :, :], xc[:, :, :], xc[:, :, :], ALU.mult).then_inc(sq_done, 1)
                pool.wait_ge(var_done, i + 1)
                pool.tensor_tensor(rstd[:, :], var[:, :], mhalf[:, :], ALU.pow).then_inc(rstd_done, 1)
                pool.wait_ge(rstd_done, i + 1)
                if not first(i):
                    pool.wait_ge(x_turned, i)
                pool.tensor_tensor(xh[:, :, :], xc[:, :, :], rstd[:, :].unsqueeze(2).broadcast_to([P, 4, C]),
                                   ALU.mult).then_inc(xh_done, 1)

            steps(pool, body)

        @block.tensor
        def _(pe):
            def hidden(i, par, g):
                if not first(i):
                    pe.wait_ge(collapsed, i * 2 + (g // 2 - 1))
                pe.matmul(psum[:, HID_BANK[g], :], w1x[:, g * 8:g * 8 + 8, :], comb_t[:, par, :],
                          start=True, stop=True).then_inc(hid_done, 1)

            def body(i, par):
                if live(i, 1):
                    pe.wait_ge(xh_done, i)
                    if not first(i, 1):
                        pe.wait_ge(lg_done, i - 1)
                    for n in range(2):
                        m = pe.transpose(psum[:, 1, n * P:n * P + P], xh[:, 2 * n:2 * n + 2, :], ident)
                    m.then_inc(x_turned, 1)
                if live(i, 0):
                    pe.wait_ge(y_staged, i + 1)
                    if not first(i):
                        pe.wait_ge(h_done, i)
                    for n in range(2):
                        m = pe.transpose(psum[:, 0, n * P:n * P + P], y_st[:, n, :], ident)
                    m.then_inc(y_turned, 1)
                if live(i, 2):
                    pe.wait_ge(mark_copied, i - 1)
                    hidden(i - 2, par, 0)
                if live(i, 1):
                    pe.wait_ge(x_copied, i)
                    for s in range(4):
                        m = pe.matmul(psum[:, 1, 256 + s * NE:256 + s * NE + NE],
                                      comb_t[0:C, 1 - par, s * P:s * P + P], rwx[:, :],
                                      start=True, stop=True, skip_group_check=True)
                    m.then_inc(logits_done, 1)
                if live(i, 2):
                    for g in range(1, 4):
                        hidden(i - 2, par, g)
                    if not first(i, 2):
                        pe.wait_ge(picked, i - 2)
                    for s in range(4):
                        m = pe.matmul(psum[:, 6, s * P:s * P + P], comb_t[:, par, s * P:s * P + P], b2x[:, :, :],
                                      start=(s == 0), stop=False, skip_group_check=True)
                if live(i, 1):
                    pe.wait_ge(chosen, i)
                    if not first(i, 1):
                        pe.wait_ge(mark_copied, i - 1)
                    for n in range(2):
                        m = pe.transpose(psum[:, 3, n * P:n * P + P], mark[:, 2 * n:2 * n + 2, :, :], ident)
                    m.then_inc(mark_turned, 1)
                if live(i, 2):
                    for g in range(2):
                        pe.wait_ge(collapsed, i * 2 + (g - 3))
                        for s in range(4):
                            m = pe.matmul(psum[:, 6, s * P:s * P + P], hid[:, g, s * P:s * P + P],
                                          w2x[:, 2 * g:2 * g + 2, :], start=False, stop=(g == 1),
                                          skip_group_check=True)
                    m.then_inc(o_done, 1)

            steps(pe, body)

        @block.scalar
        def _(act):
            def body(i, par):
                if live(i, 0):
                    if not first(i):
                        act.wait_ge(y_turned, i)
                    act.activation(y_st[:, :, :].rearrange("p k (r x) -> p k r x", r=8),
                                   raster(y, i // 2 * 512 + i % 2 * 32), ACT.Copy).then_inc(y_staged, 1)
                if live(i, 1):
                    act.wait_ge(x_turned, i)
                    if not first(i, 2):
                        act.wait_ge(o_done, i - 2)
                    for b in range(2):
                        a = act.activation(by_slot(slice(0, C), 1 - par)[:, b],
                                           psum[64 * b:64 * b + 64, 1, 0:256].rearrange("p (k q) -> p k q", k=2),
                                           ACT.Copy)
                    a.then_inc(x_copied, 1)
                if live(i, 2):
                    for g in range(2):
                        act.wait_ge(hid_done, i * 4 + (2 * g - 7))
                        if not first(i, 2):
                            act.wait_ge(o_done, i - 2)
                        act.activation(hid[:, g, :], psum[:, HID_BANK[2 * g], :], ACT.Relu).then_inc(relu_done, 1)
                if live(i, 1):
                    act.wait_ge(mark_turned, i)
                    for b in range(2):
                        a = act.activation(by_slot(slice(C, P), 1 - par)[:, b],
                                           psum[64 * b:64 * b + 64, 3, 0:256].rearrange("p (k q) -> p k q", k=2),
                                           ACT.Copy)
                    a.then_inc(mark_copied, 1)

            steps(act, body)

        @block.vector
        def _(dve):
            def body(i, par):
                if live(i, 3):
                    if not first(i, 3):
                        dve.wait_ge(out_made, i - 3)
                    dve.wait_ge(o_done, i - 2)
                    dve.tensor_reduce(best_o[:, :, :], psum[:, 6, :].rearrange("p (s g d) -> p s d g", s=4, g=2), AX.X,
                                      ALU.max).then_inc(picked, 1)
                if live(i, 0):
                    h = h_all[:, bass.ds(i * 4, 4), :]
                    dve.wait_ge(y_turned, i + 1)
                    dve.tensor_tensor(h, h, psum[:, 0, 0:256].rearrange("p (s d) -> p s d", s=4), ALU.add
                                      ).then_inc(h_done, 1)
                if live(i, 0):
                    dve.wait_ge(h_done, i + 1)
                    dve.memset(h_seen[:, :], 0.0)
                    dve.tensor_reduce(nsum[:, :], h, AX.X, ALU.add, negate=True).then_inc(nsum_done, 1)
                    dve.wait_ge(nsum_done, i + 1)
                    if not first(i):
                        dve.wait_ge(xh_done, i)
                    dve.scalar_tensor_tensor(xc[:, :, :], nsum[:, :].unsqueeze(2).broadcast_to([P, 4, C]),
                                             1.0 / C, h, ALU.mult, ALU.add).then_inc(xc_done, 1)
                if live(i, 1):
                    dve.wait_ge(logits_done, i)
                    dve.tensor_tensor(lg[:, :, :], psum[:, 1, 256:256 + 4 * NE].rearrange("p (s e) -> p s e", s=4),
                                      rb_row[:, :].unsqueeze(1).broadcast_to([P, 4, NE]), ALU.add
                                      ).then_inc(lg_done, 1)
                    dve.wait_ge(lg_done, i)
                    dve.tensor_reduce(best[:, :], lg[:, :, :], AX.X, ALU.max).then_inc(best_done, 1)
                    dve.wait_ge(best_done, i * 2 - 1)
                    dve.tensor_tensor(rank[:, :, :], lg[:, :, :], best[:, :].unsqueeze(2).broadcast_to([P, 4, NE]),
                                      ALU.is_equal).then_inc(eq_done, 1)
                if live(i, 0):
                    dve.wait_ge(sq_done, i + 1)
                    dve.tensor_reduce(ssum[:, :], sq[:, :, :], AX.X, ALU.add).then_inc(ssum_done, 1)
                if live(i, 1):
                    dve.wait_ge(eq_done, i)
                    dve.tensor_tensor(rank[:, :, :], rank[:, :, :],
                                      kc[:, K_REV:K_REV + NE].unsqueeze(1).broadcast_to([P, 4, NE]), ALU.mult
                                      ).then_inc(rank_done, 1)
                if live(i, 0):
                    dve.wait_ge(ssum_done, i + 1)
                    dve.tensor_scalar(var[:, :], ssum[:, :], 1.0 / C, LN_EPS, ALU.mult, ALU.add
                                      ).then_inc(var_done, 1)
                if live(i, 1):
                    dve.wait_ge(rank_done, i)
                    dve.tensor_reduce(best_rank[:, :], rank[:, :, :], AX.X, ALU.max).then_inc(best_done, 1)
                    dve.wait_ge(best_done, i * 2)
                    if not first(i, 1):
                        dve.wait_ge(mark_turned, i - 1)
                    dve.tensor_tensor(mark[:, :, 1, :], rank[:, :, :],
                                      best_rank[:, :].unsqueeze(2).broadcast_to([P, 4, NE]), ALU.is_equal
                                      )
                    dve.tensor_tensor(mark[:, :, 0, :], rank[:, :, :],
                                      best_rank[:, :].unsqueeze(2).broadcast_to([P, 4, NE]), ALU.not_equal
                                      ).then_inc(chosen, 1)
                if live(i, 2):
                    for g in range(2):
                        dve.wait_ge(hid_done, i * 4 + (2 * g - 6))
                        dve.wait_ge(relu_done, i * 2 + (g - 3))
                        dve.tensor_tensor(hid[:, g, :], hid[:, g, :], psum[:, HID_BANK[2 * g + 1], :], ALU.max
                                          ).then_inc(collapsed, 1)
                if live(i, 3):
                    dve.wait_ge(picked, i - 2)
                    if not first(i, 3):
                        dve.wait_ge(stored, i * 64 - 192)
                    dve.scalar_tensor_tensor(out_st[:, :, :], best_o[:, :, :], 0.0,
                                             h_all[:, bass.ds(i * 4 - 12, 4), :], ALU.max, ALU.add
                                             ).then_inc(out_made, 1)

            steps(dve, body)




_INS = ['x', 'L0_tok_qkv_w', 'L0_tok_qkv_b', 'L0_tok_proj_w', 'L0_tok_proj_b', 'L0_attn_W_dbc',
        'L0_attn_W_dt', 'L0_attn_b_dt', 'L0_attn_A_log', 'L0_attn_D', 'L0_ffn_router_w',
        'L0_ffn_router_b', 'L0_ffn_W1', 'L0_ffn_b1', 'L0_ffn_W2', 'L0_ffn_b2']


def constants():
    import numpy as np
    k = np.zeros((P, K_END), np.float32)
    k[:, K_IDENT:K_IDENT + P] = np.eye(P)
    p = np.arange(P)
    d = p % 4
    k[p ^ 1, K_SWAP + p] = 1.0
    freq = (1.0 / 10000.0 ** (np.arange(0, 4, 2, dtype=np.float32) / 4)).astype(np.float32)
    ang = np.arange(8, dtype=np.float32)[:, None] * freq
    cos, sin = np.cos(ang).astype(np.float32), np.sin(ang).astype(np.float32)
    cos4 = np.repeat(cos, 2, axis=1)
    sin4 = np.stack([-sin, sin], axis=-1).reshape(8, 4)
    k[:, K_COSC:K_COSC + 8] = cos4[:, d].T
    k[:, K_SINC:K_SINC + 8] = sin4[:, d].T
    k[:, K_COSR:K_COSR + 32] = cos4.reshape(-1)
    k[:, K_SINR:K_SINR + 32] = sin4.reshape(-1)
    k[p, K_HEAD + p % 32 // 4] = 1.0
    k[:, K_REV:K_REV + NE] = NE - np.arange(NE)
    seg = np.ones((8, TAIL), np.float32)
    seg[:, 0] = 0.0
    k[:, K_SEG:K_SEG + 8 * TAIL] = seg.reshape(-1)
    k[p, K_EYE + p % NE] = 1.0
    for w in range(2):
        k[:, K_WIN + w] = p // 32 % 2 == w
    return k


def kernel(**inputs):
    import numpy as np
    import concourse.bacc as bacc
    from concourse.bass_utils import run_bass_kernel_spmd

    nc = bacc.Bacc("TRN2", target_bir_lowering=False, num_devices=1)
    arrays, args = {}, []
    for name in _INS:
        a = np.ascontiguousarray(inputs[name])
        arrays[f"in_{name}"] = a
        args.append(nc.dram_tensor(f"in_{name}", a.shape, mybir.dt.from_np(a.dtype), kind="ExternalInput").ap())
    arrays["constants"] = constants()
    args.append(nc.dram_tensor("constants", (P, K_END), F32, kind="ExternalInput").ap())
    args.append(nc.dram_tensor("out_0", (BATCH, L, C), F32, kind="ExternalOutput").ap())
    vit_layer(nc, *args)
    r = run_bass_kernel_spmd(nc, [arrays], core_ids=[0])
    return r.results[0]["out_0"]
```
